# Optimizing a Trainium2 kernel written in Bass

```python
import numpy as np
import jax
import jax.numpy as jnp

def _softmax(x, axis=-1):
    return jax.nn.softmax(x, axis=axis)

def _gelu(x):
    return jax.nn.gelu(x, approximate=True)

def _silu(x):
    return jax.nn.silu(x)

def _sigmoid(x):
    return jax.nn.sigmoid(x)

def _layernorm(x, axis=-1, eps=1e-05):
    m = jnp.mean(x, axis=axis, keepdims=True)
    v = jnp.var(x, axis=axis, keepdims=True)
    return (x - m) / jnp.sqrt(v + eps)

def _scatter_add(tgt, idx, src, axis=0):
    return tgt.at[idx].add(src)

def _segment_sum(src, seg, n):
    return jax.ops.segment_sum(src, seg, n)
kernel_name = 'mk_adj_preln_d4_adj_r2_604ab9'

def setup_inputs(seed: int=0):
    np.random.seed(seed)
    _w = jnp.asarray

    def _rec_inputs():
        import jax
        import jax.numpy as jnp
        _gk = jax.random.key(seed)
        x = -0.000929 + 1 * jax.random.normal(jax.random.fold_in(_gk, 1), (4096, 128), jnp.float32)
        _a = jax.random.bernoulli(jax.random.fold_in(_gk, 2), 0.00390625, (4096, 4096))
        _a = jnp.logical_or(_a, jnp.swapaxes(_a, -1, -2))
        _a = jnp.logical_or(_a, jnp.eye(4096, dtype=bool))
        _af = _a.astype(jnp.float32)
        _af = _af * jax.random.uniform(jax.random.fold_in(_gk, 3), (4096, 4096), jnp.float32, 0.05, 1)
        adj = _af
        return (x, adj)
    x, adj = _rec_inputs()

    def _L0_gnn_setup():
        import jax, jax.numpy as jnp
        import numpy as np
        N = 4096
        IN_DIM = 128
        OUT_DIM = 128
        BN_EPS = 1e-05
        key = jax.random.key(seed)
        k1, k2, k3 = jax.random.split(key, 3)
        x = jax.random.normal(k1, (N, IN_DIM), dtype=jnp.float32)
        adj = jax.random.uniform(k2, (N, N), dtype=jnp.float32)
        W = jax.random.normal(k3, (IN_DIM, OUT_DIM), dtype=jnp.float32) * (1.0 / np.sqrt(IN_DIM))
        b = jnp.zeros((OUT_DIM,), dtype=jnp.float32)
        gamma = jnp.ones((OUT_DIM,), dtype=jnp.float32)
        beta = jnp.zeros((OUT_DIM,), dtype=jnp.float32)
        return {'x': x, 'adj': adj, 'W': W, 'b': b, 'gamma': gamma, 'beta': beta}
    _L0_gnn_all = _L0_gnn_setup()
    _L0_gnn_in = {k: v for k, v in _L0_gnn_all.items() if k in ('W', 'b', 'gamma', 'beta')}
    del _L0_gnn_all

    def _L1_gnn_setup():
        import jax, jax.numpy as jnp
        import numpy as np
        N = 8192
        U = 128
        AVG_DEGREE = 32
        key = jax.random.key(seed)
        kx, ka, kw = jax.random.split(key, 3)
        x = jax.random.normal(kx, (N, U), dtype=jnp.float32)
        adj = (jax.random.uniform(ka, (N, N)) < AVG_DEGREE / N).astype(jnp.float32)
        W = jax.random.normal(kw, (U, U), dtype=jnp.float32) * 0.05
        b = jnp.zeros((U,), dtype=jnp.float32)
        return {'x': x, 'adj': adj, 'W': W, 'b': b}
    _L1_gnn_all = _L1_gnn_setup()
    _L1_gnn_in = {k: v for k, v in _L1_gnn_all.items() if k in ('W', 'b')}
    del _L1_gnn_all

    def _L2_gnn_setup():
        import jax, jax.numpy as jnp
        import numpy as np
        CUTOFF = 0.5
        key = jax.random.key(seed)
        k_z, k_d, k_w, k_mu, k_sg = jax.random.split(key, 5)
        N, D_IN, D_OUT = (4096, 128, 128)
        z = jax.random.normal(k_z, (N, D_IN), dtype=jnp.float32)
        dist_matrix = jax.random.uniform(k_d, (N, N), dtype=jnp.float32)
        W = jax.random.normal(k_w, (D_IN, D_OUT), dtype=jnp.float32)
        B = jnp.zeros((D_OUT,), dtype=jnp.float32)
        mu = jax.random.normal(k_mu, (1,), dtype=jnp.float32)
        sigma = jax.random.normal(k_sg, (1,), dtype=jnp.float32)
        return {'z': z, 'dist_matrix': dist_matrix, 'W': W, 'B': B, 'mu': mu, 'sigma': sigma}
    _L2_gnn_all = _L2_gnn_setup()
    _L2_gnn_in = {k: v for k, v in _L2_gnn_all.items() if k in ('W', 'B', 'mu', 'sigma')}
    del _L2_gnn_all

    def _L3_gnn_setup():
        import jax, jax.numpy as jnp
        import numpy as np
        N = 4096
        D_IN = 128
        D_OUT = 128
        key = jax.random.key(seed)
        k1, k2, k3 = jax.random.split(key, 3)
        node_features = jax.random.normal(k1, (N, D_IN), dtype=jnp.float32)
        adj_matrix = jax.random.uniform(k2, (N, N), dtype=jnp.float32)
        limit = float(np.sqrt(6.0 / (D_IN + D_OUT)))
        weight = jax.random.uniform(k3, (D_IN, D_OUT), dtype=jnp.float32, minval=-limit, maxval=limit)
        bias = jnp.zeros((D_OUT,), dtype=jnp.float32)
        return {'node_features': node_features, 'adj_matrix': adj_matrix, 'weight': weight, 'bias': bias}
    _L3_gnn_all = _L3_gnn_setup()
    _L3_gnn_in = {k: v for k, v in _L3_gnn_all.items() if k in ('weight', 'bias')}
    del _L3_gnn_all
    return {'x': x, 'adj': adj, 'L0_gnn_W': _L0_gnn_in['W'], 'L0_gnn_b': _L0_gnn_in['b'], 'L0_gnn_gamma': _L0_gnn_in['gamma'], 'L0_gnn_beta': _L0_gnn_in['beta'], 'L1_gnn_W': _L1_gnn_in['W'], 'L1_gnn_b': _L1_gnn_in['b'], 'L2_gnn_W': _L2_gnn_in['W'], 'L2_gnn_B': _L2_gnn_in['B'], 'L2_gnn_mu': _L2_gnn_in['mu'], 'L2_gnn_sigma': _L2_gnn_in['sigma'], 'L3_gnn_weight': _L3_gnn_in['weight'], 'L3_gnn_bias': _L3_gnn_in['bias']}

def reference(x, adj, L0_gnn_W, L0_gnn_b, L0_gnn_gamma, L0_gnn_beta, L1_gnn_W, L1_gnn_b, L2_gnn_W, L2_gnn_B, L2_gnn_mu, L2_gnn_sigma, L3_gnn_weight, L3_gnn_bias):
    import jax
    import jax.numpy as jnp

    def _L0_gnn_ref(x, adj, W, b, gamma, beta):
        import jax, jax.numpy as jnp
        import numpy as np
        N = 4096
        IN_DIM = 128
        OUT_DIM = 128
        BN_EPS = 1e-05
        rowsum = adj.sum(axis=1)
        d_inv_sqrt = jax.lax.rsqrt(rowsum + 1e-06)
        adj_norm = adj * d_inv_sqrt[:, None] * d_inv_sqrt[None, :]
        support = x @ W + b
        out = adj_norm @ support
        mean = out.mean(axis=0)
        var = out.var(axis=0)
        out = (out - mean) * jax.lax.rsqrt(var + BN_EPS) * gamma + beta
        out = jax.nn.relu(out)
        return out

    def _L1_gnn_ref(x, adj, W, b):
        import jax, jax.numpy as jnp
        import numpy as np
        N = 8192
        U = 128
        AVG_DEGREE = 32
        adj = jax.lax.stop_gradient(adj)
        neigh1 = adj @ x
        x1 = jax.nn.swish(neigh1 @ W + b)
        neigh2 = adj @ x1
        x2 = jax.nn.swish(neigh2 @ W + b)
        return x2

    def _L2_gnn_ref(z, dist_matrix, W, B, mu, sigma):
        import jax, jax.numpy as jnp
        import numpy as np
        CUTOFF = 0.5
        N = dist_matrix.shape[0]
        h = z @ W + B
        mask = (dist_matrix < CUTOFF) & ~jnp.eye(N, dtype=bool)
        r = jnp.where(mask, dist_matrix, 1.0)
        sens = jnp.exp(-(1.0 / r - 1.0 / mu[0]) ** 2 / (2.0 * sigma[0] ** 2))
        S = jnp.where(mask, sens, 0.0)
        return S @ h

    def _L3_gnn_ref(node_features, adj_matrix, weight, bias):
        import jax, jax.numpy as jnp
        import numpy as np
        N = 4096
        D_IN = 128
        D_OUT = 128
        n = adj_matrix.shape[0]
        a_hat = adj_matrix + jnp.eye(n, dtype=adj_matrix.dtype)
        d_hat = jnp.sum(a_hat, axis=1)
        d_inv_sqrt = jnp.where(d_hat > 0, jax.lax.rsqrt(d_hat), 0.0)
        adj_normalized = d_inv_sqrt[:, None] * a_hat * d_inv_sqrt[None, :]
        support = node_features @ weight
        out = adj_normalized @ support + bias
        return out
    h = jnp.maximum(_layernorm(x, axis=-1), 0.0)
    x = x + _L0_gnn_ref(h, adj, L0_gnn_W, L0_gnn_b, L0_gnn_gamma, L0_gnn_beta)
    h = jnp.maximum(_layernorm(x, axis=-1), 0.0)
    x = x + _L1_gnn_ref(h, adj, L1_gnn_W, L1_gnn_b)
    h = jnp.maximum(_layernorm(x, axis=-1), 0.0)
    x = x + _L2_gnn_ref(h, adj, L2_gnn_W, L2_gnn_B, L2_gnn_mu, L2_gnn_sigma)
    h = jnp.maximum(_layernorm(x, axis=-1), 0.0)
    x = x + _L3_gnn_ref(h, adj, L3_gnn_weight, L3_gnn_bias)
    return x

_drawn_inputs = setup_inputs


def setup_inputs(seed=0):
    import zlib

    import numpy as np

    out = dict(_drawn_inputs(seed))
    spreads = {'L0_gnn_b': (0.0, 0.689),
     'L0_gnn_gamma': (1.0, 0.2),
     'L0_gnn_beta': (0.0, 0.1),
     'L1_gnn_b': (0.0, 0.1),
     'L2_gnn_B': (0.0, 2.0),
     'L3_gnn_bias': (0.0, 0.8)}
    factors = {'L2_gnn_W': 21.625}
    for name, (base, spread) in spreads.items():
        noise = np.random.default_rng([zlib.crc32(name.encode()), seed]).standard_normal(out[name].shape)
        drawn = base * np.exp(spread * noise) if base else spread * noise
        out[name] = jnp.asarray(drawn.astype(out[name].dtype))
    for name, factor in factors.items():
        out[name] = (out[name] * factor).astype(out[name].dtype)
    return out
```

```python
import concourse.bass as bass
from concourse import mybir
from contextlib import ExitStack

P = 128
N = 4096
PANEL = 512
NP = N // PANEL
B = PANEL // P
NBLK = N // P
TILE_SLOTS = 8
S_SLOTS = 3
Y_SLOTS = 2
MAIN_BANKS, CHAIN_BANKS, SMALL_BANKS = 3, 2, 3
IN, L0, L1A, L1B, L2, L3 = "input", 0, 1, 2, 3, 4
LN_EPS = 1e-5
BN_EPS = 1e-5
DEG_EPS = 1e-6
TINY = 1e-18
CUTOFF = 0.5

STAGES = {
    IN: [(0, "norm"), (1, "transpose"), (1, "support")],
    "degree": [(1, "fold"), (3, "degree_row")],
    "batch_norm": [(0, "bn_apply"), (0, "untranspose"), (0, "norm")],
    L1A: [(1, "dense")],
    L1B: [(1, "dense"), (2, "norm"), (4, "transpose"), (5, "support")],
    L2: [(1, "untranspose"), (1, "norm")],
    L3: [(1, "dense")],
}
MAKES = {("degree", "fold"): (L0, 2), ("batch_norm", "norm"): (L1A, 1), (L1A, "dense"): (L1B, 1),
         (L1B, "support"): (L2, 1), (L2, "norm"): (L3, 2)}


def sweeps():
    up = range(NP)
    fresh_last = lambda i, rest: [*range(i - 1), *rest, *range(max(i - 1, 0), i)]
    rows = [(i, j, False, j <= i) for i in up for j in fresh_last(i, range(i + 1, NP)) + [i]]
    l0 = [(i, j, True, False) for i in up for j in range(i + 1, NP)]
    l1a = [(i, j, True, j < i) for i in up for j in fresh_last(i, range(i, NP))]
    turn = [(1, 1), (2, 2), (0, 0), (1, 0), (2, 1), (2, 0)]
    turn += [(i, j) for i in range(3, NP) for j in fresh_last(i, [i])]
    l1b = [(NP - 1 - i, NP - 1 - j, True, j < i) for i, j in turn]
    l2 = [(i, j, True, j < i) for i, j in turn]
    l3 = [(i, j, True, False) for i in up for j in range(i, NP)]
    return [(None, L0, rows), (L0, None, l0), (L1A, L1B, l1a), (L1B, L2, l1b), (L2, L3, l2), (L3, None, l3)]


class Step:

    def __init__(self, kind, layer=None, i=0, j=0, visit=None, k=None, e=None, bank=None, bank_uses=0, bank_free=0,
                 group=None, first=False, last=False, operand=None, products=0, ready=None, stages=None,
                 norm=None, ev=None, ev_free=0, rows=None, rows_free=0, ht=None, ht_free=0, ht_e=None,
                 support=None, diag_free=0, acc_free=0, chain_count=0, main_count=0, n=None, diagonal=False, used=0,
                 job=None, store_free=0):
        self.kind, self.layer = kind, layer
        self.i, self.j, self.visit = i, j, visit
        self.k = k
        self.e, self.bank, self.bank_uses = e, bank, bank_uses
        self.group, self.bank_free = group, bank_free
        self.first, self.last = first, last
        self.operand, self.ready = operand, ready
        self.products, self.stages = products, stages
        self.norm = norm
        self.ev, self.ev_free = ev, ev_free
        self.rows, self.rows_free = rows, rows_free
        self.ht, self.ht_free, self.ht_e = ht, ht_free, ht_e
        self.support, self.diag_free, self.acc_free = support, diag_free, acc_free
        self.chain_count, self.main_count = chain_count, main_count
        self.n, self.diagonal, self.used = n, diagonal, used
        self.job, self.store_free = job, store_free


class Planner:
    def __init__(self):
        self.steps, self.visits = [], []
        self.tick = 0
        self.count = dict.fromkeys(["product", "main", "chain", "small", "norm", "result"], 0)
        self.readers = {"ev": [], "rows": [], "ht": []}
        self.open = []
        self.late = []
        self.made_by, self.due, self.maker, self.made = {}, {}, {}, {}
        self.silu_norms = []
        self.groups, self.bank_user, self.partial = {}, {}, set()
        self.size = {}

    def emit(self, kind, **fields):
        self.steps.append(Step(kind, **fields))
        return self.steps[-1]

    def small(self, kind, **fields):
        e = self.count["small"]
        self.count["small"] += 1
        return self.emit(kind, e=e, bank=e % SMALL_BANKS, bank_uses=e // SMALL_BANKS, **fields)

    def take(self, buffer):
        readers = self.readers[buffer]
        readers.append(None)
        n = len(readers) - 1
        return {buffer: n, buffer + "_free": readers[n - 2] + 1 if n >= 2 else 0}

    def stage(self, panel):
        _, what = panel.stages.pop(0)
        layer, i = panel.layer, panel.i
        if what == "dense":
            s = self.small("dense", layer=layer, i=i, ev=panel.ev, ready=panel.ready)
            self.readers["ev"][panel.ev] = s.e
            made_by = ("small", s.e)
            if layer == L1B:
                panel.silu = s.silu = len(self.silu_norms)
                panel.silu_e = s.e
                s.silu_free = self.silu_norms[s.silu - 2] + 1 if s.silu >= 2 else 0
                self.silu_norms.append(None)
            if layer == L3:
                s.result, s.bias3 = self.count["result"], self.made["bias3"]
                self.count["result"] += 1
        elif what == "untranspose":
            panel.e = self.small("untranspose", layer=layer, i=i, ev=panel.ev, ready=panel.ready).e
            self.readers["ev"][panel.ev] = panel.e
        elif what == "bn_apply":
            ev = self.take("ev")
            panel.ev, panel.ready = ev["ev"], ("bn_applied", i + 1)
            self.emit("bn_apply", i=i, **ev)
        elif what == "norm":
            s = self.emit("norm", layer=layer, i=i, norm=self.count["norm"], rows=None, e=None)
            self.count["norm"] += 1
            if layer in (IN, L1B):
                half = self.take("rows")
                panel.rows, s.rows, s.rows_free = half["rows"], half["rows"], half["rows_free"]
            if layer in ("batch_norm", L2):
                s.e = panel.e
            if layer == L1B:
                s.silu, s.silu_e = panel.silu, panel.silu_e
                self.silu_norms[s.silu] = s.norm
            panel.norm = s.norm
            made_by = ("norm", s.norm)
        elif what == "transpose":
            s = self.small("transpose", layer=layer, i=i, rows=panel.rows, norm=panel.norm, **self.take("ht"))
            self.readers["rows"][panel.rows] = s.e
            panel.ht, panel.ht_e = s.ht, s.e
        elif what == "support":
            s = self.small("support", layer=layer, i=i, ht=panel.ht, ht_e=panel.ht_e)
            self.readers["ht"][panel.ht] = s.e
            made_by = ("small", s.e)
            if layer == IN:
                self.made["support", i] = s.e
        elif what == "fold":
            self.made["fold", i] = self.small("fold", i=i, support=self.made["support", i],
                                              diag_free=self.made.get(("degree_row", i - 1), -1) + 1).e
            made_by = ("pool", i)
        elif what == "degree_row":
            panel.e = self.small("degree_row", i=i).e
            self.made["degree_row", i] = panel.e
        if (layer, what) in MAKES:
            of, time = MAKES[layer, what]
            self.made_by[of, i] = made_by
            self.due[of, i] = self.tick + time

    def begin(self, layer, i, start, **fields):
        panel = Step("panel", layer=layer, i=i, stages=[(start + d, w) for d, w in STAGES[layer]], **fields)
        self.open.append(panel)
        for _, what in panel.stages:
            if (layer, what) in MAKES:
                self.maker[MAKES[layer, what][0], i] = panel
        return panel

    def run_due(self):
        for panel in self.open:
            while panel.stages and panel.stages[0][0] <= self.tick:
                self.stage(panel)
        self.open = [p for p in self.open if p.stages]
        for late in self.late:
            v, layer, i, j = late
            if self.due.get((layer, j), 1 << 30) <= self.tick or v <= len(self.visits) - TILE_SLOTS + 2:
                self.late.remove(late)
                self.product(v, layer, i, j, "chain")
                return self.run_due()

    def need(self, layer, j):
        maker = self.maker[layer, j]
        while (layer, j) not in self.made_by:
            for panel in self.open:
                if panel.stages:
                    self.stage(panel)
                    break
            assert maker.stages or (layer, j) in self.made_by

    def product(self, v, layer, i, j, kind):
        self.need(layer, j)
        key = (kind, layer, i)
        if key not in self.groups:
            taken = {g.bank for k, g in self.groups.items() if k[0] == kind}
            free = set(range(MAIN_BANKS if kind == "main" else CHAIN_BANKS)) - taken
            bank = min(free, key=lambda b: self.bank_user.get((kind, b), 0))
            self.groups[key] = Step("group", bank=bank, products=0, bank_free=self.bank_user.get((kind, bank), 0))
        g = self.groups[key]
        g.products += 1
        last = g.products == self.size[key]
        k = self.count["product"]
        self.emit("product", k=k, visit=v, layer=layer, i=i, j=j, group=kind, bank=g.bank, first=g.products == 1,
                  last=last, bank_free=g.bank_free, operand=self.made_by[layer, j])
        self.count["product"] += 1
        self.tick += 1
        if not last:
            return
        del self.groups[key]
        n = self.count[kind]
        self.count[kind] += 1
        self.bank_user[kind, g.bank] = n + 1
        if kind == "chain":
            self.emit("chain_evacuate", layer=layer, i=i, bank=g.bank, k=k, main_count=self.count["main"])
            self.partial.add((layer, i))
            self.made["partial", layer, i] = n + 1
        elif layer == L0:
            self.emit("layer0_evacuate", i=i, bank=g.bank, k=k, chain_count=self.made["partial", layer, i],
                      e=self.made["degree_row", i])
        else:
            ev = self.take("ev")
            self.emit("main_evacuate", layer=layer, i=i, bank=g.bank, k=k,
                      chain_count=self.made.get(("partial", layer, i), 0), **ev)
            self.begin(layer, i, self.tick, ready=("main", n), **ev)

    def radial_steps(self):
        uses = [s for s in self.steps if s.kind == "product" and s.layer == L2]
        for n, s in enumerate(uses):
            s.s = n
        after = {}
        front_at = []
        for n, s in enumerate(uses):
            front = max(uses[n - S_SLOTS].k if n >= S_SLOTS else 0, s.k - 6,
                        front_at[n - Y_SLOTS][1] if n >= Y_SLOTS else 0)
            back = max(front, s.k - 3, front_at[-1][1] if front_at else 0)
            front_at.append((front, back))
            f = dict(n=n, visit=s.visit, diagonal=s.i == s.j, used=uses[n - S_SLOTS].k + 1 if n >= S_SLOTS else 0)
            after.setdefault(front, []).append(Step("radial_front", **f))
            after.setdefault(back, []).append(Step("radial_back", **f))
        steps = []
        for s in self.steps:
            steps.append(s)
            if s.kind == "product":
                steps += sorted(after.get(s.k, []), key=lambda r: r.n + (1.5 if r.kind == "radial_back" else 0))
        self.steps = steps
        diagonals = 0
        for s in self.steps:
            if s.kind == "radial_back" and s.diagonal:
                diagonals += 1
                uses[s.n].diagonals = diagonals

    def tile_uses(self):
        first, last = {}, {}
        for v in self.visits:
            v.k = v.radial = v.added = 0
        for t, s in enumerate(self.steps):
            if s.kind in ("product", "row_add", "radial_front", "radial_back"):
                v = self.visits[s.visit]
                if s.kind == "product" and s.layer != L2:
                    v.k = s.k + 1
                elif s.kind == "row_add":
                    v.added = s.visit + 1
                elif s.kind == "radial_back":
                    v.radial = s.n + 1
                if s.kind != "product" or s.layer != L2:
                    first.setdefault(s.visit, t)
                    last[s.visit] = t
        free = 0
        for v in range(TILE_SLOTS, len(self.visits)):
            free = max(free, last[v - TILE_SLOTS])
            assert free < first[v], ("a tile is kept too long", v)

    def run(self):
        all_sweeps = sweeps()
        for main, chain, tiles in all_sweeps:
            for i, _, m, ch in tiles:
                for key, on in ((("main", main, i), m), (("chain", chain, i), ch)):
                    self.size[key] = self.size.get(key, 0) + on
        for n, (main, chain, tiles) in enumerate(all_sweeps):
            if chain == L0:
                for i in range(NP):
                    self.begin(IN, i, 3 * i)
            if main == L1A:
                while self.late:
                    self.tick += 1
                    self.run_due()
                self.emit("layer0_evacuate", i=NP - 1, bank=None, k=None,
                          chain_count=self.made["partial", L0, NP - 1], e=self.made["degree_row", NP - 1])
                self.made["bias3"] = self.small("batch_norm").e
                for i in range(NP):
                    self.begin("batch_norm", i, self.tick + i - 2)
            for i, j, m, ch in tiles:
                v = len(self.visits)
                self.visits.append(Step("visit", i=i, j=j))
                if chain == L0:
                    self.emit("row_add", visit=v, i=i, first=v % NP == 0,
                              acc_free=self.made.get(("fold", i - 2), -1) + 1)
                    if j == i:
                        self.begin("degree", i, self.tick)
                if m:
                    self.product(v, main, i, j, "main")
                if ch:
                    if self.due.get((chain, j), 1 << 30) <= self.tick:
                        self.product(v, chain, i, j, "chain")
                    else:
                        self.late.append((v, chain, i, j))
                elif chain == L0:
                    self.tick += 1
                self.run_due()
            if chain == L0:
                while self.late:
                    self.tick += 1
                    self.run_due()
                self.emit("layer3_degrees", e=self.made["fold", NP - 1])
        while self.open or self.late:
            self.tick += 1
            self.run_due()
        self.radial_steps()
        self.tile_uses()
        return self.steps, self.visits


def graph_layers_kernel(nc, x_in, adj_in, w0, b0, gamma, beta, w1, b1, w2, b2, mu, sigma, w3, b3, out):
    fp32 = mybir.dt.float32
    ACT = mybir.ActivationFunctionType
    ALU = mybir.AluOpType
    steps, visits = Planner().run()

    with ExitStack() as ctx:
        def sb(name, shape):
            return ctx.enter_context(nc.sbuf_tensor(name, shape, fp32))

        def sem(name):
            return ctx.enter_context(nc.semaphore(name))

        tiles = sb("tiles", [P, TILE_SLOTS, B, PANEL])
        weights = sb("weights", [P, S_SLOTS, B, PANEL])
        recips = sb("recips", [P, Y_SLOTS, B, PANEL])
        x = sb("x", [P, NBLK, P])
        operands = [sb("operand_a", [P, NBLK, P]), sb("operand_b", [P, NBLK, P])]
        partial = sb("partial", [P, NP, PANEL])
        row_acc = recips
        degree_rows = weights[:, 0:2].rearrange("p s b n -> p (s b) n")
        operand_of = {L0: operands[1], L1A: operands[0], L1B: operands[1], L2: operands[0], L3: operands[1]}
        support0 = operands[0]
        sums_t = sb("sums_t", [P, 2, PANEL])
        rows = sb("rows", [P, 2, B, P])
        rows_t = sb("rows_t", [P, 2, PANEL])
        silu = sb("silu", [P, 2, B, P])
        scratch = sb("scratch", [P, 2, B, P])
        diag = sb("diag", [P, B, P])
        w_sb = sb("w_sb", [P, 4, P])
        row_vec = sb("row_vec", [1, 4, P])
        col_vec = sb("col_vec", [P, 2])
        radial_in = sb("radial_in", [1, 2])
        radial = sb("radial", [P, 6])
        ident = sb("ident", [P, P])
        ones = sb("ones", [P, P])
        bias3 = sb("bias3", [P, P])
        tiny = sb("tiny", [P, 1])
        minus_half = sb("minus_half", [P, NBLK])
        row_sum = sb("row_sum", [P, NBLK])
        deg_in = sb("deg_in", [P, NBLK])
        d0 = sb("d0", [P, NBLK])
        deg3_in = sb("deg3_in", [P, 2, NBLK])
        d3 = sb("d3", [P, NBLK])
        ln_stats = sb("ln_stats", [P, B, 6])
        ln_mv = sb("ln_mv", [P, B, 2])
        ln_var = sb("ln_var", [P, 2, B])
        ln_rstd = sb("ln_rstd", [P, 2, B])
        ln_scale = sb("ln_scale", [P, B])
        bn_stats = sb("bn_stats", [P, NP, 6])
        bn_mv = sb("bn_mv", [P, 2])
        bn_var = sb("bn_var", [P, 1])
        bn_rstd = sb("bn_rstd", [P, 1])
        bn_affine = sb("bn_affine", [P, 3])

        def psum(name):
            return ctx.enter_context(nc.psum_tensor(name, [P, PANEL], fp32))

        banks = {"main": [psum(f"main_{b}") for b in range(MAIN_BANKS)],
                 "chain": [psum(f"chain_{b}") for b in range(CHAIN_BANKS)]}
        small = [psum(f"small_{b}") for b in range(SMALL_BANKS)]

        def by_block(ap):
            return ap.rearrange("p (b n) -> p b n", b=B)

        tile_loaded = [sem(f"tile_loaded_{s}") for s in range(TILE_SLOTS)]
        x_loaded = sem("x_loaded")
        consts_loaded = sem("consts_loaded")
        zeroed = sem("zeroed")
        consts_made = sem("consts_made")
        bias3_taken = sem("bias3_taken")
        products_done = sem("products_done")
        small_done = sem("small_done")
        small_taken = [sem(f"small_taken_{b}") for b in range(SMALL_BANKS)]
        main_taken = sem("main_taken")
        chain_taken = sem("chain_taken")
        rows_added = sem("rows_added")
        layer0_out = sem("layer0_out")
        bn_applied = sem("bn_applied")
        normed = sem("normed")
        variance_ready = sem("variance_ready")
        rstd_ready = sem("rstd_ready")
        degree_ready = sem("degree_ready")
        operand0_ready = sem("operand0_ready")
        diag_ready = sem("diag_ready")
        degree3_in_ready = sem("degree3_in_ready")
        degree3_raw = sem("degree3_raw")
        bn_variance_ready = sem("bn_variance_ready")
        bn_rstd_ready = sem("bn_rstd_ready")
        bn_affine_ready = sem("bn_affine_ready")
        radial_ready = sem("radial_ready")
        recip_seeded = sem("recip_seeded")
        recip_done = sem("recip_done")
        exp_done = sem("exp_done")
        weights_masked = sem("weights_masked")
        diagonal_cleared = sem("diagonal_cleared")
        stored = [sem("stored_0"), sem("stored_1")]
        act_order = sem("act_order")
        dve_order = sem("dve_order")

        consts = [(row_vec[0:1, n, :], v.rearrange("(a n) -> a n", a=1)) for n, v in enumerate([b0, b1, b2, b3])]
        consts += [(col_vec[:, n:n + 1], v.rearrange("(n a) -> n a", a=1)) for n, v in enumerate([gamma, beta])]
        consts += [(radial_in[0:1, n:n + 1], v.rearrange("(a n) -> a n", a=1)) for n, v in enumerate([mu, sigma])]
        consts += [(w_sb[:, n, :], w[:, :]) for n, w in enumerate([w0, w1, w2, w3])]
        CONSTS_LOADED = 16 * len(consts)
        CONSTS_MADE = 4

        def wait_loaded(engine, v):
            engine.wait_ge(tile_loaded[v % TILE_SLOTS], 16 * (v // TILE_SLOTS + 1))

        def wait_taken(engine, e):
            engine.wait_ge(small_taken[e % SMALL_BANKS], e // SMALL_BANKS + 1)

        block = ctx.enter_context(nc.Block())

        @block.sync
        def _(sp):
            sp.dma_start(x[:, :, :], x_in.rearrange("(b p) f -> p b f", p=P)).then_inc(x_loaded, 16)
            for n, v in enumerate(visits):
                if n >= TILE_SLOTS:
                    old = visits[n - TILE_SLOTS]
                    if old.k:
                        sp.wait_ge(products_done, old.k)
                    if old.added:
                        sp.wait_ge(rows_added, old.added)
                    if old.radial:
                        sp.wait_ge(weights_masked, old.radial)
                sp.dma_start(tiles[:, n % TILE_SLOTS, :, :], adj_in[v.i, v.j, :, :, :])\
                    .then_inc(tile_loaded[n % TILE_SLOTS], 16)

        @block.gpsimd
        def _(pool):
            nc.gpsimd.memset(ident[:, :], 0.0).then_inc(zeroed, 1)
            nc.gpsimd.memset(ones[:, :], 1.0).then_inc(consts_made, 1)
            nc.gpsimd.memset(tiny[:, :], TINY).then_inc(consts_made, 1)
            nc.gpsimd.memset(minus_half[:, :], -0.5).then_inc(consts_made, 1)
            pool.wait_ge(zeroed, 1)
            nc.gpsimd.affine_select(out=ident[:, :], in_=ident[:, :], compare_op=ALU.not_equal, fill=1.0, base=0,
                                    pattern=[[-1, P]], channel_multiplier=1).then_inc(consts_made, 1)
            pool.wait_ge(consts_made, CONSTS_MADE)
            for s in steps:
                if s.kind == "norm":
                    h = s.norm % 2
                    pool.wait_ge(variance_ready, s.norm + 1)
                    nc.gpsimd.tensor_tensor(ln_rstd[:, h, :], ln_var[:, h, :], minus_half[:, 0:B], ALU.pow)\
                        .then_inc(rstd_ready, 1)
                elif s.kind == "fold":
                    blocks = slice(B * s.i, B * s.i + B)
                    wait_taken(pool, s.e)
                    nc.gpsimd.tensor_tensor(d0[:, blocks], deg_in[:, blocks], minus_half[:, 0:B], ALU.pow)\
                        .then_inc(degree_ready, 1)
                    pool.wait_ge(degree_ready, s.i + 1)
                    wait_taken(pool, s.support)
                    d = d0[:, blocks].unsqueeze(2).broadcast_to([P, B, P])
                    nc.gpsimd.tensor_tensor(operand_of[L0][:, blocks, :], support0[:, blocks, :], d, ALU.mult)\
                        .then_inc(operand0_ready, 1)
                    if s.i:
                        pool.wait_ge(small_done, s.diag_free)
                    nc.gpsimd.tensor_tensor(diag[:, :, :], ident[:, :].unsqueeze(1).broadcast_to([P, B, P]), d,
                                            ALU.mult).then_inc(diag_ready, 1)
                elif s.kind == "layer3_degrees":
                    pool.wait_ge(degree3_in_ready, 1)
                    nc.gpsimd.tensor_tensor(d3[:, :], deg3_in[:, 0, :], minus_half[:, :], ALU.pow)\
                        .then_inc(degree3_raw, 1)
                elif s.kind == "batch_norm":
                    pool.wait_ge(bn_variance_ready, 1)
                    nc.gpsimd.tensor_tensor(bn_rstd[:, :], bn_var[:, :], minus_half[:, 0:1], ALU.pow)\
                        .then_inc(bn_rstd_ready, 1)
                elif s.kind == "radial_back" and s.diagonal:
                    pool.wait_ge(weights_masked, s.n + 1)
                    w = weights[:, s.n % S_SLOTS, :, :]
                    nc.gpsimd.affine_select(out=w, in_=w, compare_op=ALU.not_equal, fill=0.0, base=0,
                                            pattern=[[-P, B], [1, PANEL]], channel_multiplier=-1)\
                        .then_inc(diagonal_cleared, 1)

        @block.scalar
        def _(act):
            order = [0]

            def then(ins):
                order[0] += 1
                ins.then_inc(act_order, 1)
                act.wait_ge(act_order, order[0])

            for to, frm in consts:
                act.dma_start(to, frm).then_inc(consts_loaded, 16)
            act.wait_ge(consts_made, CONSTS_MADE)
            for s in steps:
                if s.kind in ("transpose", "support", "degree_row") or s.kind == "dense" and s.layer != L3:
                    act.wait_ge(small_done, s.e + 1)
                blocks = slice(B * s.i, B * s.i + B)
                if s.kind == "chain_evacuate":
                    act.wait_ge(products_done, s.k + 1)
                    if s.main_count:
                        act.wait_ge(main_taken, s.main_count)
                    nc.scalar.activation(partial[:, s.i, :], banks["chain"][s.bank][:, :], ACT.Copy)\
                        .then_inc(chain_taken, 1)
                elif s.kind == "transpose":
                    if s.ht_free:
                        act.wait_ge(small_done, s.ht_free)
                    nc.scalar.activation(rows_t[:, s.ht % 2, :], small[s.bank][:, :], ACT.Copy)\
                        .then_inc(small_taken[s.bank], 1)
                elif s.kind == "support":
                    to = support0 if s.layer == IN else operand_of[L2]
                    nc.scalar.activation(to[:, blocks, :], by_block(small[s.bank][:, :]), ACT.Copy)\
                        .then_inc(small_taken[s.bank], 1)
                elif s.kind == "degree_row":
                    nc.scalar.activation(degree_rows[:, s.i, :], small[s.bank][:, :], ACT.Copy)\
                        .then_inc(small_taken[s.bank], 1)
                elif s.kind == "bn_apply":
                    act.wait_ge(bn_affine_ready, 1)
                    if s.ev_free:
                        act.wait_ge(small_done, s.ev_free)
                    nc.scalar.activation(sums_t[:, s.ev % 2, :], partial[:, s.i, :], ACT.Relu,
                                         scale=bn_affine[:, 0:1], bias=bn_affine[:, 2:3]).then_inc(bn_applied, 1)
                elif s.kind == "dense" and s.layer == L1A:
                    nc.scalar.activation(operand_of[L1B][:, blocks, :], by_block(small[s.bank][:, :]), ACT.Silu)\
                        .then_inc(small_taken[s.bank], 1)
                elif s.kind == "dense" and s.layer == L1B:
                    if s.silu_free:
                        act.wait_ge(normed, s.silu_free)
                    nc.scalar.activation(silu[:, s.silu % 2, :, :], by_block(small[s.bank][:, :]), ACT.Silu)\
                        .then_inc(small_taken[s.bank], 1)
                elif s.kind == "dense" and s.layer == L3:
                    wait_taken(act, s.e)
                    act.dma_start(out[PANEL * s.i:PANEL * s.i + PANEL, :].rearrange("(b p) f -> p b f", p=P),
                                  scratch[:, s.result % 2, :, :]).then_inc(stored[s.result % 2], 16)
                elif s.kind == "radial_front":
                    y = recips[:, s.n % Y_SLOTS, :, :]
                    wait_loaded(act, s.visit)
                    if s.n >= Y_SLOTS:
                        act.wait_ge(weights_masked, s.n - Y_SLOTS + 1)
                    if s.n == 0:
                        act.wait_ge(radial_ready, 1)
                    then(nc.scalar.activation(y, tiles[:, s.visit % TILE_SLOTS, :, :], ACT.Ln, bias=tiny[:, 0:1]))
                    nc.scalar.activation(y, y, ACT.Exp, scale=-1.0).then_inc(recip_seeded, 1)
                elif s.kind == "radial_back":
                    y = recips[:, s.n % Y_SLOTS, :, :]
                    act.wait_ge(recip_done, s.n + 1)
                    then(nc.scalar.activation(y, y, ACT.Square, bias=radial[:, 2:3]))
                    nc.scalar.activation(y, y, ACT.Exp, scale=radial[:, 5:6]).then_inc(exp_done, 1)
            act.wait_ge(stored[0], 16 * (NP // 2))
            act.wait_ge(stored[1], 16 * (NP // 2))

        @block.vector
        def _(dve):
            order = [0]

            def then(ins):
                order[0] += 1
                ins.then_inc(dve_order, 1)
                dve.wait_ge(dve_order, order[0])

            def over_blocks(ap):
                return ap.unsqueeze(2).broadcast_to([P, B, P])

            def layer_norm(s, to):
                h = s.norm % 2
                xs = x[:, B * s.i:B * s.i + B, :]
                for b in range(B):
                    last = nc.vector.bn_stats(ln_stats[:, b, :], xs[:, b, :])
                then(last)
                for b in range(B):
                    last = nc.vector.bn_aggr(ln_mv[:, b, :], ln_stats[:, b, :])
                then(last)
                nc.vector.tensor_scalar(ln_var[:, h, :], ln_mv[:, :, 1], LN_EPS, None, ALU.add)\
                    .then_inc(variance_ready, 1)
                then(nc.vector.tensor_tensor(scratch[:, h, :, :], xs, over_blocks(ln_mv[:, :, 0]), ALU.subtract))
                dve.wait_ge(rstd_ready, s.norm + 1)
                scale = ln_rstd[:, h, :]
                if s.layer == L2:
                    then(nc.vector.tensor_tensor(ln_scale[:, :], scale, d3[:, B * s.i:B * s.i + B], ALU.mult))
                    scale = ln_scale[:, :]
                nc.vector.scalar_tensor_tensor(out=to, in0=scratch[:, h, :, :], scalar=0.0, in1=over_blocks(scale),
                                               op0=ALU.max, op1=ALU.mult).then_inc(normed, 1)

            dve.wait_ge(x_loaded, 16)
            dve.wait_ge(consts_made, CONSTS_MADE)
            for s in steps:
                blocks = slice(B * s.i, B * s.i + B)
                if s.kind == "row_add":
                    acc = row_acc[:, s.i % 2, :, :]
                    wait_loaded(dve, s.visit)
                    tile = tiles[:, s.visit % TILE_SLOTS, :, :]
                    if s.first:
                        if s.i >= 2:
                            dve.wait_ge(small_done, s.acc_free)
                        nc.vector.tensor_copy(acc, tile).then_inc(rows_added, 1)
                    else:
                        dve.wait_ge(rows_added, s.visit)
                        nc.vector.tensor_tensor(acc, acc, tile, ALU.add).then_inc(rows_added, 1)
                elif s.kind == "fold":
                    dve.wait_ge(small_done, s.e + 1)
                    sums = small[s.bank][:, 0:B]
                    nc.vector.tensor_copy(row_sum[:, blocks], sums)
                    nc.vector.tensor_scalar(deg_in[:, blocks], sums, DEG_EPS, None, ALU.add)\
                        .then_inc(small_taken[s.bank], 1)
                elif s.kind == "layer3_degrees":
                    wait_taken(dve, s.e)
                    then(nc.vector.tensor_scalar(deg3_in[:, 0, :], row_sum[:, :], 1.0, None, ALU.add))
                    then(nc.vector.tensor_scalar(deg3_in[:, 1, :], deg3_in[:, 0, :], 0.0, None, ALU.is_gt))
                    nc.vector.tensor_scalar(deg3_in[:, 0, :], deg3_in[:, 0, :], 1e-30, None, ALU.max)\
                        .then_inc(degree3_in_ready, 1)
                    dve.wait_ge(degree3_raw, 1)
                    then(nc.vector.tensor_tensor(d3[:, :], d3[:, :], deg3_in[:, 1, :], ALU.mult))
                elif s.kind == "layer0_evacuate":
                    part = partial[:, s.i, :]
                    dve.wait_ge(chain_taken, s.chain_count)
                    if s.k is not None:
                        dve.wait_ge(products_done, s.k + 1)
                        nc.vector.tensor_tensor(part, banks["main"][s.bank][:, :], part, ALU.add)\
                            .then_inc(main_taken, 1)
                        dve.wait_ge(main_taken, s.i + 1)
                    wait_taken(dve, s.e)
                    then(nc.vector.tensor_tensor(part, part, degree_rows[:, s.i, :], ALU.mult))
                    nc.vector.bn_stats(bn_stats[:, s.i, :], part).then_inc(layer0_out, 1)
                elif s.kind == "batch_norm":
                    dve.wait_ge(layer0_out, NP)
                    then(nc.vector.bn_aggr(bn_mv[:, :], bn_stats[:, :, :].rearrange("p n s -> p (n s)")))
                    nc.vector.tensor_scalar(bn_var[:, :], bn_mv[:, 1:2], BN_EPS, None, ALU.add)\
                        .then_inc(bn_variance_ready, 1)
                    dve.wait_ge(bn_rstd_ready, 1)
                    dve.wait_ge(consts_loaded, CONSTS_LOADED)
                    then(nc.vector.tensor_tensor(bn_affine[:, 0:1], bn_rstd[:, :], col_vec[:, 0:1], ALU.mult))
                    then(nc.vector.tensor_tensor(bn_affine[:, 1:2], bn_mv[:, 0:1], bn_affine[:, 0:1], ALU.mult))
                    nc.vector.tensor_tensor(bn_affine[:, 2:3], col_vec[:, 1:2], bn_affine[:, 1:2], ALU.subtract)\
                        .then_inc(bn_affine_ready, 1)
                    dve.wait_ge(small_done, s.e + 1)
                    then(nc.vector.tensor_copy(radial[:, 0:2], small[s.bank][:, P:P + 2]))
                    then(nc.vector.reciprocal(radial[:, 2:3], radial[:, 0:1]))
                    then(nc.vector.tensor_scalar(radial[:, 3:4], radial[:, 1:2], radial[:, 1:2], -2.0, ALU.mult, ALU.mult))
                    then(nc.vector.reciprocal(radial[:, 5:6], radial[:, 3:4]))
                    nc.vector.tensor_copy(radial[:, 4:5], radial[:, 5:6]).then_inc(radial_ready, 1)
                    nc.vector.tensor_copy(bias3[:, :], small[s.bank][:, 0:P]).then_inc(small_taken[s.bank], 1)
                elif s.kind == "main_evacuate":
                    dve.wait_ge(products_done, s.k + 1)
                    if s.ev_free:
                        dve.wait_ge(small_done, s.ev_free)
                    to = sums_t[:, s.ev % 2, :]
                    if s.chain_count:
                        dve.wait_ge(chain_taken, s.chain_count)
                        nc.vector.tensor_tensor(to, banks["main"][s.bank][:, :], partial[:, s.i, :], ALU.add)\
                            .then_inc(main_taken, 1)
                    else:
                        nc.vector.tensor_copy(to, banks["main"][s.bank][:, :]).then_inc(main_taken, 1)
                elif s.kind == "norm":
                    xs = x[:, blocks, :]
                    if s.e is not None:
                        dve.wait_ge(small_done, s.e + 1)
                        nc.vector.tensor_tensor(xs, xs, by_block(small[s.e % SMALL_BANKS][:, :]), ALU.add)\
                            .then_inc(small_taken[s.e % SMALL_BANKS], 1)
                        wait_taken(dve, s.e)
                    if s.layer == L1B:
                        wait_taken(dve, s.silu_e)
                        then(nc.vector.tensor_tensor(xs, xs, silu[:, s.silu % 2, :, :], ALU.add))
                    if s.rows is not None:
                        if s.rows_free:
                            dve.wait_ge(small_done, s.rows_free)
                        layer_norm(s, rows[:, s.rows % 2, :, :])
                    else:
                        layer_norm(s, operand_of[L1A if s.layer == "batch_norm" else L3][:, blocks, :])
                elif s.kind == "dense" and s.layer == L3:
                    xs = x[:, blocks, :]
                    if s.result == 0:
                        wait_taken(dve, s.bias3)
                    then(nc.vector.tensor_tensor(xs, xs, bias3[:, :].unsqueeze(1).broadcast_to([P, B, P]), ALU.add))
                    dve.wait_ge(small_done, s.e + 1)
                    if s.result >= 2:
                        dve.wait_ge(stored[s.result % 2], 16 * (s.result // 2))
                    for b in range(B):
                        n = B * s.i + b
                        last = nc.vector.scalar_tensor_tensor(
                            out=scratch[:, s.result % 2, b, :], in0=small[s.bank][:, b * P:b * P + P],
                            scalar=d3[:, n:n + 1], in1=x[:, n, :], op0=ALU.mult, op1=ALU.add)
                    last.then_inc(small_taken[s.bank], 1)
                elif s.kind == "radial_front":
                    y = recips[:, s.n % Y_SLOTS, :, :]
                    t = weights[:, s.n % S_SLOTS, :, :]
                    dve.wait_ge(recip_seeded, s.n + 1)
                    if s.used:
                        dve.wait_ge(products_done, s.used)
                    then(nc.vector.tensor_tensor(t, tiles[:, s.visit % TILE_SLOTS, :, :], y, ALU.mult))
                    flat = lambda a: a.rearrange("p b n -> p (b n)")
                    nc.vector.scalar_tensor_tensor(out=flat(y), in0=flat(t), scalar=2.0, in1=flat(y),
                                                   op0=ALU.subtract, op1=ALU.mult).then_inc(recip_done, 1)
                elif s.kind == "radial_back":
                    dve.wait_ge(exp_done, s.n + 1)
                    nc.vector.scalar_tensor_tensor(
                        out=weights[:, s.n % S_SLOTS, :, :], in0=tiles[:, s.visit % TILE_SLOTS, :, :], scalar=CUTOFF,
                        in1=recips[:, s.n % Y_SLOTS, :, :], op0=ALU.is_lt, op1=ALU.mult).then_inc(weights_masked, 1)

        @block.tensor
        def _(pe):
            def wait_operand(made_by):
                what, n = made_by
                if what == "small":
                    wait_taken(pe, n)
                elif what == "norm":
                    pe.wait_ge(normed, n + 1)
                elif what == "pool":
                    pe.wait_ge(operand0_ready, n + 1)

            def wait_sums(ready):
                what, n = ready
                if what == "main":
                    pe.wait_ge(main_taken, n + 1)
                else:
                    pe.wait_ge(bn_applied, n)

            pe.wait_ge(consts_made, CONSTS_MADE)
            pe.wait_ge(consts_loaded, CONSTS_LOADED)
            for s in steps:
                if s.bank_uses:
                    pe.wait_ge(small_taken[s.bank], s.bank_uses)
                if s.kind == "product":
                    if s.layer == L2:
                        pe.wait_ge(weights_masked, s.s + 1)
                        if s.i == s.j:
                            pe.wait_ge(diagonal_cleared, s.diagonals)
                        moving = weights[:, s.s % S_SLOTS, :, :]
                    else:
                        wait_loaded(pe, s.visit)
                        moving = tiles[:, s.visit % TILE_SLOTS, :, :]
                    wait_operand(s.operand)
                    if s.first and s.bank_free:
                        pe.wait_ge(main_taken if s.group == "main" else chain_taken, s.bank_free)
                    bank = banks[s.group][s.bank]
                    for b in range(B):
                        last = nc.tensor.matmul(bank[:, :], operand_of[s.layer][:, B * s.j + b, :], moving[:, b, :],
                                                start=s.first and b == 0, stop=s.last and b == B - 1)
                        if s.layer == L3 and s.i == s.j and b == 0:
                            for c in range(B):
                                nc.tensor.matmul(bank[:, c * P:c * P + P], operand_of[L3][:, B * s.j + c, :],
                                                 ident[:, :], start=False, stop=False)
                    last.then_inc(products_done, 1)
                elif s.kind == "dense":
                    wait_sums(s.ready)
                    for b in range(B):
                        to = small[s.bank][:, b * P:b * P + P]
                        last = nc.tensor.matmul(to, sums_t[:, s.ev % 2, b * P:b * P + P],
                                                w_sb[:, 3 if s.layer == L3 else 1, :], start=True, stop=s.layer == L3)
                        if s.layer != L3:
                            last = nc.tensor.matmul(to, ones[0:1, :], row_vec[0:1, 1, :], start=False, stop=True)
                    last.then_inc(small_done, 1)
                elif s.kind == "untranspose":
                    wait_sums(s.ready)
                    for b in range(B):
                        last = nc.tensor.transpose(small[s.bank][:, b * P:b * P + P],
                                                   sums_t[:, s.ev % 2, b * P:b * P + P], ident[:, :])
                    last.then_inc(small_done, 1)
                elif s.kind == "transpose":
                    pe.wait_ge(normed, s.norm + 1)
                    for b in range(B):
                        last = nc.tensor.transpose(small[s.bank][:, b * P:b * P + P], rows[:, s.rows % 2, b, :],
                                                   ident[:, :])
                    last.then_inc(small_done, 1)
                elif s.kind == "support":
                    wait_taken(pe, s.ht_e)
                    w = 0 if s.layer == IN else 2
                    for b in range(B):
                        to = small[s.bank][:, b * P:b * P + P]
                        nc.tensor.matmul(to, rows_t[:, s.ht % 2, b * P:b * P + P], w_sb[:, w, :],
                                         start=True, stop=False)
                        last = nc.tensor.matmul(to, ones[0:1, :], row_vec[0:1, w, :], start=False, stop=True)
                    last.then_inc(small_done, 1)
                elif s.kind == "fold":
                    pe.wait_ge(rows_added, NP * (s.i + 1))
                    for b in range(B):
                        for c in range(B):
                            last = nc.tensor.matmul(small[s.bank][:, b:b + 1],
                                                    row_acc[:, s.i % 2, c, b * P:b * P + P], ones[:, 0:1],
                                                    start=c == 0, stop=c == B - 1)
                    last.then_inc(small_done, 1)
                elif s.kind == "degree_row":
                    pe.wait_ge(diag_ready, s.i + 1)
                    nc.tensor.matmul(small[s.bank][:, :], ones[:, :], diag[:, :, :].rearrange("p b n -> p (b n)"),
                                     start=True, stop=True).then_inc(small_done, 1)
                elif s.kind == "batch_norm":
                    nc.tensor.matmul(small[s.bank][:, 0:P], ones[0:1, :], row_vec[0:1, 3, :], start=True, stop=True)
                    nc.tensor.matmul(small[s.bank][:, P:P + 2], ones[0:1, :], radial_in[0:1, :],
                                     start=True, stop=True).then_inc(small_done, 1)


_INS = ["x", "adj", "L0_gnn_W", "L0_gnn_b", "L0_gnn_gamma", "L0_gnn_beta", "L1_gnn_W", "L1_gnn_b", "L2_gnn_W",
        "L2_gnn_B", "L2_gnn_mu", "L2_gnn_sigma", "L3_gnn_weight", "L3_gnn_bias"]
_OUTS = [((4096, 128), "float32")]


def kernel(**inputs):
    import numpy as _np
    import concourse.bacc as _bacc
    from concourse import mybir as _mybir
    from concourse.bass_utils import run_bass_kernel_spmd as _run

    nc = _bacc.Bacc("TRN2", target_bir_lowering=False, num_devices=1)
    arrays, args = {}, []
    for name in _INS:
        a = _np.ascontiguousarray(inputs[name])
        if name == "adj":
            a = _np.ascontiguousarray(a.reshape(NP, PANEL, NP, B, P).transpose(0, 2, 4, 3, 1))
        arrays[f"in_{name}_dram"] = a
        args.append(nc.dram_tensor(f"in_{name}_dram", a.shape, _mybir.dt.from_np(a.dtype), kind="ExternalInput").ap())
    for i, (shape, dtype) in enumerate(_OUTS):
        dt = _mybir.dt.from_np(_np.dtype(dtype))
        args.append(nc.dram_tensor(f"out_{i}_dram", shape, dt, kind="ExternalOutput").ap())
    graph_layers_kernel(nc, *args)
    r = _run(nc, [arrays], core_ids=[0])
    got = tuple(r.results[0][f"out_{i}_dram"] for i in range(len(_OUTS)))
    return got[0]
```

```python
import concourse.bass as bass
from concourse import mybir
from contextlib import ExitStack

P = 128
N = 4096
PANEL = 512
NP = N // PANEL
B = PANEL // P
NBLK = N // P
TILE_SLOTS = 9
S_SLOTS = 3
KEEP_AT, USE_AT = (0, 1, 2, 3), (-8, -6, -5, -3)
KEPT_LOAD_AHEAD = 8
KEEP_GAP = 0
Y_SLOTS = 2
MAIN_BANKS, CHAIN_BANKS, SMALL_BANKS = 3, 2, 3
IN, L0, L1A, L1B, L2, L3 = "input", 0, 1, 2, 3, 4
LN_EPS = 1e-5
BN_EPS = 1e-5
DEG_EPS = 1e-6
TINY = 1e-18
CUTOFF = 0.5
SUPPORT_AT = 3
X_REST_AT = 3
BURST = 1


def kept_in_dram(i, j):
    return (i + j) % 2 == 0

STAGES = {
    IN: [(0, "norm"), (1, "scale"), (2, "transpose"), (3, "support")],
    "degree": [(1, "fold"), (5, "degree_row")],
    "batch_norm": [(0, "bn_apply"), (1, "untranspose"), (1, "norm"), (2, "scale")],
    L1A: [(2, "dense")],
    L1B: [(1, "dense"), (2, "norm"), (4, "transpose"), (5, "support")],
    L2: [(1, "untranspose"), (1, "norm")],
    L3: [(1, "dense")],
}
MAKES = {("degree", "fold"): (L0, 2), ("batch_norm", "scale"): (L1A, 1), (L1A, "dense"): (L1B, 1),
         (L1B, "support"): (L2, 1), (L2, "norm"): (L3, 2)}


def sweeps():
    up = range(NP)
    fresh_last = lambda i, rest: [*range(i - 1), *rest, *range(max(i - 1, 0), i)]
    rows = [(i, j, False, j <= i) for i in up for j in fresh_last(i, range(i + 1, NP)) + [i]]
    l0 = [(i, j, True, False) for i in up for j in range(i + 1, NP)]
    l1a = [(i, j, True, False) for j in up for i in (0, 1)] + [(1, 0, False, True)]
    l1a += [(i, j, True, j < i) for i in range(2, NP) for j in fresh_last(i, range(i, NP))]
    turn = [(1, 1), (2, 2), (0, 0), (1, 0), (2, 1), (2, 0)]
    turn += [(i, j) for i in range(3, NP) for j in fresh_last(i, [i])]
    l1b = [(NP - 1 - i, NP - 1 - j, True, j < i) for i, j in turn]
    l2 = [(i, j, True, j < i) for i, j in turn]
    l3 = [(i, j, True, False) for i in up for j in range(i, NP)]
    return [(None, L0, rows), (L0, None, l0), (L1A, L1B, l1a), (L1B, L2, l1b), (L2, L3, l2), (L3, None, l3)]


class Step:

    def __init__(self, kind, layer=None, i=0, j=0, visit=None, k=None, e=None, bank=None, bank_uses=0, bank_free=0,
                 group=None, first=False, last=False, operand=None, products=0, ready=None, stages=None,
                 norm=None, ev=None, ev_free=0, rows=None, rows_free=0, ht=None, ht_free=0, ht_e=None,
                 support=None, diag_free=0, acc_free=0, chain_count=0, main_count=0, n=None, diagonal=False, used=0,
                 job=None, store_free=0):
        self.kind, self.layer = kind, layer
        self.i, self.j, self.visit = i, j, visit
        self.k = k
        self.e, self.bank, self.bank_uses = e, bank, bank_uses
        self.group, self.bank_free = group, bank_free
        self.first, self.last = first, last
        self.operand, self.ready = operand, ready
        self.products, self.stages = products, stages
        self.norm = norm
        self.ev, self.ev_free = ev, ev_free
        self.rows, self.rows_free = rows, rows_free
        self.ht, self.ht_free, self.ht_e = ht, ht_free, ht_e
        self.support, self.diag_free, self.acc_free = support, diag_free, acc_free
        self.chain_count, self.main_count = chain_count, main_count
        self.n, self.diagonal, self.used = n, diagonal, used
        self.job, self.store_free = job, store_free


class Planner:
    def __init__(self):
        self.steps, self.visits = [], []
        self.tick = 0
        self.count = dict.fromkeys(["product", "main", "chain", "small", "norm", "first_norms", "result"], 0)
        self.readers = {"ev": [], "rows": [], "ht": []}
        self.open = []
        self.late = []
        self.made_by, self.due, self.made = {}, {}, {}
        self.silu_norms = []
        self.bursts = False
        self.groups, self.bank_user = {}, {}
        self.size = {}

    def emit(self, kind, **fields):
        self.steps.append(Step(kind, **fields))
        return self.steps[-1]

    def small(self, kind, **fields):
        e = self.count["small"]
        self.count["small"] += 1
        return self.emit(kind, e=e, bank=e % SMALL_BANKS, bank_uses=e // SMALL_BANKS, **fields)

    def take(self, buffer):
        readers = self.readers[buffer]
        readers.append(None)
        n = len(readers) - 1
        return {buffer: n, buffer + "_free": readers[n - 2] + 1 if n >= 2 else 0}

    def stage(self, panel):
        _, what = panel.stages.pop(0)
        layer, i = panel.layer, panel.i
        if what == "dense":
            s = self.small("dense", layer=layer, i=i, ev=panel.ev, ready=panel.ready)
            self.readers["ev"][panel.ev] = s.e
            made_by = ("small", s.e)
            if layer == L1B:
                panel.silu = s.silu = len(self.silu_norms)
                panel.silu_e = s.e
                s.silu_free = self.silu_norms[s.silu - 2] + 1 if s.silu >= 2 else 0
                self.silu_norms.append(None)
            if layer == L3:
                s.result, s.bias3 = self.count["result"], self.made["bias3"]
                self.count["result"] += 1
        elif what == "untranspose":
            panel.e = self.small("untranspose", layer=layer, i=i, ev=panel.ev, ready=panel.ready).e
            self.readers["ev"][panel.ev] = panel.e
        elif what == "bn_apply":
            ev = self.take("ev")
            panel.ev, panel.ready = ev["ev"], ("bn_applied", i + 1)
            self.emit("bn_apply", i=i, **ev)
        elif what == "norm":
            s = self.emit("norm", layer=layer, i=i, norm=self.count["norm"], rows=None, e=None)
            self.count["norm"] += 1
            if layer == L1B:
                half = self.take("rows")
                panel.rows, s.rows, s.rows_free = half["rows"], half["rows"], half["rows_free"]
            if layer in ("batch_norm", L2):
                s.e = panel.e
            if layer == L1B:
                s.silu, s.silu_e = panel.silu, panel.silu_e
                self.silu_norms[s.silu] = s.norm
            panel.norm = s.norm
            made_by = ("norm", s.norm)
        elif what == "scale":
            s = self.emit("scale", layer=layer, i=i, norm=panel.norm)
            s.first_norms = self.count["first_norms"]
            self.count["first_norms"] += 1
            if layer == IN:
                half = self.take("rows")
                panel.rows, s.rows, s.rows_free = half["rows"], half["rows"], half["rows_free"]
            made_by = ("norm", panel.norm)
        elif what == "transpose":
            s = self.small("transpose", layer=layer, i=i, rows=panel.rows, norm=panel.norm, **self.take("ht"))
            self.readers["rows"][panel.rows] = s.e
            panel.ht, panel.ht_e = s.ht, s.e
        elif what == "support":
            s = self.small("support", layer=layer, i=i, ht=panel.ht, ht_e=panel.ht_e)
            self.readers["ht"][panel.ht] = s.e
            made_by = ("small", s.e)
            if layer == IN:
                self.made["support", i] = s.e
        elif what == "fold":
            self.made["fold", i] = self.small("fold", i=i, support=self.made["support", i],
                                              diag_free=self.made.get(("degree_row", i - 1), -1) + 1).e
            made_by = ("pool", i)
        elif what == "degree_row":
            panel.e = self.small("degree_row", i=i).e
            self.made["degree_row", i] = panel.e
        if (layer, what) in MAKES:
            of, time = MAKES[layer, what]
            self.made_by[of, i] = made_by
            self.due[of, i] = self.tick + time

    def begin(self, layer, i, start, **fields):
        panel = Step("panel", layer=layer, i=i, stages=[(start + d, w) for d, w in STAGES[layer]], **fields)
        self.open.append(panel)
        return panel

    def run_due(self):
        for panel in self.open:
            while panel.stages and panel.stages[0][0] <= self.tick:
                self.stage(panel)
        self.open = [p for p in self.open if p.stages]
        ready = [t for t in self.late if self.due.get((t[1], t[3]), 1 << 30) <= self.tick]
        kept = [t for t in self.late if t[0] <= len(self.visits) - TILE_SLOTS + 2]
        if kept or len(ready) >= (BURST if self.bursts else 1):
            for t in ready + [t for t in kept if t not in ready]:
                self.late.remove(t)
                self.product(*t, "chain")
            self.run_due()

    def take_until(self, made, what):
        while what not in made:
            self.stage(next(panel for panel in self.open if panel.stages))

    def need(self, layer, j):
        self.take_until(self.made_by, (layer, j))

    def product(self, v, layer, i, j, kind):
        self.need(layer, j)
        key = (kind, layer, i)
        if key not in self.groups:
            taken = {g.bank for k, g in self.groups.items() if k[0] == kind}
            free = set(range(MAIN_BANKS if kind == "main" else CHAIN_BANKS)) - taken
            bank = min(free, key=lambda b: self.bank_user.get((kind, b), 0))
            self.groups[key] = Step("group", bank=bank, products=0, bank_free=self.bank_user.get((kind, bank), 0))
        g = self.groups[key]
        g.products += 1
        last = g.products == self.size[key]
        k = self.count["product"]
        self.emit("product", k=k, visit=v, layer=layer, i=i, j=j, group=kind, bank=g.bank, first=g.products == 1,
                  last=last, bank_free=g.bank_free, operand=self.made_by[layer, j])
        self.count["product"] += 1
        self.tick += 1
        if not last:
            return
        del self.groups[key]
        n = self.count[kind]
        self.count[kind] += 1
        self.bank_user[kind, g.bank] = n + 1
        if kind == "chain":
            self.emit("chain_evacuate", layer=layer, i=i, bank=g.bank, k=k, main_count=self.count["main"])
            self.made["partial", layer, i] = n + 1
            if (layer, i) == (L0, NP - 1):
                self.take_until(self.made, ("degree_row", i))
                self.emit("layer0_evacuate", i=i, chain_count=n + 1, e=self.made["degree_row", i])
        elif layer == L0:
            self.take_until(self.made, ("degree_row", i))
            self.emit("layer0_evacuate", i=i, bank=g.bank, k=k, chain_count=self.made["partial", layer, i],
                      e=self.made["degree_row", i])
        else:
            ev = self.take("ev")
            self.emit("main_evacuate", layer=layer, i=i, bank=g.bank, k=k,
                      chain_count=self.made.get(("partial", layer, i), 0), **ev)
            self.begin(layer, i, self.tick, ready=("main", n), **ev)

    def radial_steps(self):
        products = [s for s in self.steps if s.kind == "product"]
        keeps = [s for s in products if s.layer == L1A and kept_in_dram(s.i, s.j)]
        uses = [s for s in products if s.layer == L2]
        at = {}
        seeds, masks, freed, before = [], [], [], 0
        counts = {"masked": 0, "cleared": 0}
        slot_loads, slot_stores = [0] * S_SLOTS, [0] * S_SLOTS
        stored = {}

        def place(k, order, step):
            at.setdefault(k, []).append((order, step))

        for n, s in enumerate(keeps + uses):
            keep, slot = s.layer == L1A, n % S_SLOTS
            fields = dict(n=n, visit=s.visit, i=s.i, j=s.j)
            free = freed[n - S_SLOTS] if n >= S_SLOTS else (0, None)
            before = max(before, free[0])
            if keep or not kept_in_dram(s.i, s.j):
                m = len(masks)
                ahead = KEEP_AT if keep else USE_AT
                seed = max(s.k + ahead[0], seeds[-1] + KEEP_GAP if keep and seeds else 0, masks[m - Y_SLOTS] if m >= Y_SLOTS else 0, seeds[-1] if seeds else 0)
                newton = max(s.k + ahead[1], seed + 1, before)
                exp = max(s.k + ahead[2], newton + 1)
                mask = max(s.k + ahead[3], exp + 1)
                seeds.append(seed)
                masks.append(mask)
                before = newton
                counts["masked"] += 1
                counts["cleared"] += s.i == s.j
                ready = ("masked", counts["masked"], counts["cleared"] if s.i == s.j else 0)
                for kind, k, order in (("radial_seed", seed, n), ("radial_newton", newton, n + 0.1),
                                       ("radial_exp", exp, n + 1.4), ("radial_mask", mask, n + 1.5)):
                    step = Step(kind, **fields)
                    step.m, step.free, step.ready = m, free[1], ready
                    place(k, order, step)
                if keep:
                    slot_stores[slot] += 1
                    step = Step("radial_store", **fields)
                    step.ready = ready
                    place(mask + 1, n + 1.7, step)
                    stored[s.i, s.j] = (slot, slot_stores[slot])
                    freed.append((mask + 1, ("stored", slot, slot_stores[slot])))
            else:
                slot_loads[slot] += 1
                before = max(before, s.k - KEPT_LOAD_AHEAD)
                step = Step("radial_load", **fields)
                step.free, step.stored = free[1], stored[s.i, s.j]
                place(before, n, step)
                ready = ("loaded", slot, slot_loads[slot])
            if not keep:
                s.n, s.ready = n, ready
                freed.append((s.k, ("used", s.k + 1)))
        steps, due = [], []
        for s in self.steps:
            if s.kind == "product":
                steps += due
                due = [step for _, step in sorted(at.get(s.k, []), key=lambda t: t[0])]
            steps.append(s)
        self.steps = steps + due

    def tile_loads(self):
        first, last = {}, {}
        for v in self.visits:
            v.k = v.radial = v.added = 0
        for t, s in enumerate(self.steps):
            uses_tile = s.kind in ("row_add", "radial_seed", "radial_newton", "radial_mask") or s.kind == "product" and s.layer != L2
            if not uses_tile:
                continue
            v = self.visits[s.visit]
            if s.kind == "product":
                v.k = s.k + 1
            elif s.kind == "row_add":
                v.added = s.visit + (1 if s.n else 2)
            elif s.kind == "radial_mask":
                v.radial = s.ready[1]
            first.setdefault(s.visit, t)
            last[s.visit] = t
        loads, at = {}, -1
        for v in range(len(self.visits)):
            if v >= TILE_SLOTS:
                at = max(at, last.get(v - TILE_SLOTS, -1))
                if v in first:
                    assert at < first[v], ("a tile is kept too long", v)
            loads.setdefault(at, []).append(v)
        steps = [Step("load", visit=v) for v in loads.get(-1, [])]
        for t, s in enumerate(self.steps):
            steps.append(s)
            steps += [Step("load", visit=v) for v in loads.get(t, [])]
        self.steps = steps

    def run(self):
        all_sweeps = sweeps()
        for main, chain, tiles in all_sweeps:
            for i, _, m, ch in tiles:
                for key, on in ((("main", main, i), m), (("chain", chain, i), ch)):
                    self.size[key] = self.size.get(key, 0) + on
        for n, (main, chain, tiles) in enumerate(all_sweeps):
            if chain == L0:
                for i in range(NP):
                    self.begin(IN, i, i if i < 2 else NP * (i - 1) + SUPPORT_AT)
            if main == L1A:
                self.emit("layer3_degrees", e=self.made["fold", NP - 1])
                self.made["bias3"] = self.small("batch_norm").e
                for i in range(NP):
                    self.begin("batch_norm", i, self.tick + i)
                while (L1A, 0) not in self.made_by:
                    self.run_due()
                    self.tick += 1
            self.bursts = chain == L0
            self.run_due()
            for i, j, m, ch in tiles:
                v = len(self.visits)
                self.visits.append(Step("visit", i=i, j=j))
                if chain == L0:
                    self.emit("row_add", visit=v, i=i, n=v % NP, last=v % NP == NP - 1,
                              acc_free=self.made.get(("fold", i - 2), -1) + 1)
                    if j == i:
                        self.begin("degree", i, self.tick)
                if m:
                    self.product(v, main, i, j, "main")
                if ch:
                    if self.due.get((chain, j), 1 << 30) <= self.tick and not self.bursts:
                        self.product(v, chain, i, j, "chain")
                    else:
                        self.late.append((v, chain, i, j))
                if chain == L0:
                    self.tick += 1
                self.run_due()
        while self.open or self.late:
            self.tick += 1
            self.run_due()
        self.radial_steps()
        self.tile_loads()
        return self.steps, self.visits


def graph_layers_kernel(nc, x_in, adj_in, w0, b0, gamma, beta, w1, b1, w2, b2, mu, sigma, w3, b3, out):
    fp32 = mybir.dt.float32
    ACT = mybir.ActivationFunctionType
    ALU = mybir.AluOpType
    steps, visits = Planner().run()

    with ExitStack() as ctx:
        def sb(name, shape):
            return ctx.enter_context(nc.sbuf_tensor(name, shape, fp32))

        def sem(name):
            return ctx.enter_context(nc.semaphore(name))

        kept = nc.dram_tensor("kept_weights", [NP, NP, P, B, PANEL], fp32, kind="Internal").ap()
        tiles = sb("tiles", [P, TILE_SLOTS, B, PANEL])
        weights = sb("weights", [P, S_SLOTS, B, PANEL])
        recips = sb("recips", [P, Y_SLOTS, B, PANEL])
        x = sb("x", [P, NBLK, P])
        operands = [sb("operand_a", [P, NBLK, P]), sb("operand_b", [P, NBLK, P])]
        partial = sb("partial", [P, NP, PANEL])
        row_acc = recips
        degree_rows = weights[:, 0:2].rearrange("p s b n -> p (s b) n")
        operand_of = {L0: operands[1], L1A: operands[0], L1B: operands[1], L2: operands[0], L3: operands[1]}
        support0 = operands[0]
        sums_t = sb("sums_t", [P, 2, PANEL])
        rows = sb("rows", [P, 2, B, P])
        rows_t = sb("rows_t", [P, 2, PANEL])
        silu = sb("silu", [P, 2, B, P])
        scratch = sb("scratch", [P, 2, B, P])
        diag = sb("diag", [P, B, P])
        w_sb = sb("w_sb", [P, 4, P])
        row_vec = sb("row_vec", [1, 4, P])
        col_vec = sb("col_vec", [P, 2])
        radial_in = sb("radial_in", [1, 2])
        radial = sb("radial", [P, 6])
        ident = sb("ident", [P, P])
        ones = sb("ones", [P, P])
        bias3 = sb("bias3", [P, P])
        tiny = sb("tiny", [P, 1])
        minus_half = sb("minus_half", [P, NBLK])
        row_sum = sb("row_sum", [P, NBLK])
        deg_in = sb("deg_in", [P, NBLK])
        d0 = sb("d0", [P, NBLK])
        deg3_in = sb("deg3_in", [P, 2, NBLK])
        d3 = sb("d3", [P, NBLK])
        ln_stats = sb("ln_stats", [P, B, 6])
        ln_mv = sb("ln_mv", [P, B, 2])
        ln_var = sb("ln_var", [P, 2, B])
        ln_negmean = sb("ln_negmean", [P, 2, B])
        ln_rstd = sb("ln_rstd", [P, 2, B])
        ln_scale = sb("ln_scale", [P, B])
        ln_shift = sb("ln_shift", [P, 2, B])
        bn_stats = sb("bn_stats", [P, NP, 6])
        bn_mv = sb("bn_mv", [P, 2])
        bn_var = sb("bn_var", [P, 1])
        bn_rstd = sb("bn_rstd", [P, 1])
        bn_affine = sb("bn_affine", [P, 3])

        def psum(name):
            return ctx.enter_context(nc.psum_tensor(name, [P, PANEL], fp32))

        banks = {"main": [psum(f"main_{b}") for b in range(MAIN_BANKS)],
                 "chain": [psum(f"chain_{b}") for b in range(CHAIN_BANKS)]}
        small = [psum(f"small_{b}") for b in range(SMALL_BANKS)]

        def by_block(ap):
            return ap.rearrange("p (b n) -> p b n", b=B)

        tile_loaded = [sem(f"tile_loaded_{s}") for s in range(TILE_SLOTS)]
        x_loaded = [sem("x_loaded_first"), sem("x_loaded_rest")]
        first_consts_loaded = sem("first_consts_loaded")
        consts_loaded = sem("consts_loaded")
        zeroed = sem("zeroed")
        consts_made = sem("consts_made")
        bias3_taken = sem("bias3_taken")
        products_done = sem("products_done")
        small_done = sem("small_done")
        small_taken = [sem(f"small_taken_{b}") for b in range(SMALL_BANKS)]
        main_taken = sem("main_taken")
        chain_taken = sem("chain_taken")
        rows_added = sem("rows_added")
        blocks_added = sem("blocks_added")
        layer0_out = sem("layer0_out")
        bn_applied = sem("bn_applied")
        normed = sem("normed")
        variance_ready = sem("variance_ready")
        rstd_ready = sem("rstd_ready")
        shift_ready = sem("shift_ready")
        degree_ready = sem("degree_ready")
        operand0_ready = sem("operand0_ready")
        diag_ready = sem("diag_ready")
        degree3_in_ready = sem("degree3_in_ready")
        degree3_raw = sem("degree3_raw")
        bn_variance_ready = sem("bn_variance_ready")
        bn_rstd_ready = sem("bn_rstd_ready")
        bn_affine_ready = sem("bn_affine_ready")
        radial_ready = sem("radial_ready")
        recip_seeded = sem("recip_seeded")
        recip_done = sem("recip_done")
        exp_done = sem("exp_done")
        weights_masked = sem("weights_masked")
        diagonal_cleared = sem("diagonal_cleared")
        weights_stored = [sem(f"weights_stored_{s}") for s in range(S_SLOTS)]
        weights_loaded = [sem(f"weights_loaded_{s}") for s in range(S_SLOTS)]
        stored = [sem("stored_0"), sem("stored_1")]
        act_order = sem("act_order")
        dve_order = sem("dve_order")

        first_consts = [(w_sb[:, 0, :], w0[:, :]), (row_vec[0:1, 0, :], b0.rearrange("(a n) -> a n", a=1))]
        consts = [(row_vec[0:1, n, :], v.rearrange("(a n) -> a n", a=1)) for n, v in ((1, b1), (2, b2), (3, b3))]
        consts += [(col_vec[:, n:n + 1], v.rearrange("(n a) -> n a", a=1)) for n, v in enumerate([gamma, beta])]
        consts += [(radial_in[0:1, n:n + 1], v.rearrange("(a n) -> a n", a=1)) for n, v in enumerate([mu, sigma])]
        consts += [(w_sb[:, n, :], w[:, :]) for n, w in ((1, w1), (2, w2), (3, w3))]
        CONSTS_LOADED = 16 * len(consts)
        CONSTS_MADE = 4

        def wait_loaded(engine, v):
            engine.wait_ge(tile_loaded[v % TILE_SLOTS], 16 * (v // TILE_SLOTS + 1))

        def wait_taken(engine, e):
            engine.wait_ge(small_taken[e % SMALL_BANKS], e // SMALL_BANKS + 1)

        def wait_slot_free(engine, free):
            if free is None:
                return
            if free[0] == "stored":
                engine.wait_ge(weights_stored[free[1]], 16 * free[2])
            else:
                engine.wait_ge(products_done, free[1])

        def wait_weights(engine, ready):
            if ready[0] == "loaded":
                engine.wait_ge(weights_loaded[ready[1]], 16 * ready[2])
            else:
                engine.wait_ge(weights_masked, ready[1])
                if ready[2]:
                    engine.wait_ge(diagonal_cleared, ready[2])

        block = ctx.enter_context(nc.Block())

        @block.sync
        def _(sp):
            sp.dma_start(x[:, 0:2 * B, :], x_in[:, 0:2 * B, :]).then_inc(x_loaded[0], 16)
            for s in steps:
                if s.kind == "load":
                    n, v = s.visit, visits[s.visit]
                    if n == X_REST_AT:
                        sp.dma_start(x[:, 2 * B:NBLK, :], x_in[:, 2 * B:NBLK, :]).then_inc(x_loaded[1], 16)
                    if n >= TILE_SLOTS:
                        old = visits[n - TILE_SLOTS]
                        if old.k:
                            sp.wait_ge(products_done, old.k)
                        if old.added:
                            sp.wait_ge(rows_added, old.added)
                        if old.radial:
                            sp.wait_ge(weights_masked, old.radial)
                    sp.dma_start(tiles[:, n % TILE_SLOTS, :, :], adj_in[v.i, v.j, :, :, :])\
                        .then_inc(tile_loaded[n % TILE_SLOTS], 16)
                elif s.kind == "radial_load":
                    sp.wait_ge(weights_stored[s.stored[0]], 16 * s.stored[1])
                    wait_slot_free(sp, s.free)
                    sp.dma_start(weights[:, s.n % S_SLOTS, :, :], kept[s.i, s.j, :, :, :])\
                        .then_inc(weights_loaded[s.n % S_SLOTS], 16)

        @block.gpsimd
        def _(pool):
            nc.gpsimd.memset(ident[:, :], 0.0).then_inc(zeroed, 1)
            nc.gpsimd.memset(ones[:, :], 1.0).then_inc(consts_made, 1)
            nc.gpsimd.memset(tiny[:, :], TINY).then_inc(consts_made, 1)
            nc.gpsimd.memset(minus_half[:, :], -0.5).then_inc(consts_made, 1)
            pool.wait_ge(zeroed, 1)
            nc.gpsimd.affine_select(out=ident[:, :], in_=ident[:, :], compare_op=ALU.not_equal, fill=1.0, base=0,
                                    pattern=[[-1, P]], channel_multiplier=1).then_inc(consts_made, 1)
            pool.wait_ge(consts_made, CONSTS_MADE)
            for s in steps:
                if s.kind == "norm":
                    h = s.norm % 2
                    pool.wait_ge(variance_ready, s.norm + 1)
                    nc.gpsimd.tensor_tensor(ln_rstd[:, h, :], ln_var[:, h, :], minus_half[:, 0:B], ALU.pow)\
                        .then_inc(rstd_ready, 1)
                    if s.layer in (IN, "batch_norm"):
                        pool.wait_ge(rstd_ready, s.norm + 1)
                        nc.gpsimd.tensor_tensor(ln_shift[:, h, :], ln_negmean[:, h, :], ln_rstd[:, h, :], ALU.mult)\
                            .then_inc(shift_ready, 1)
                elif s.kind == "fold":
                    blocks = slice(B * s.i, B * s.i + B)
                    wait_taken(pool, s.e)
                    nc.gpsimd.tensor_tensor(d0[:, blocks], deg_in[:, blocks], minus_half[:, 0:B], ALU.pow)\
                        .then_inc(degree_ready, 1)
                    pool.wait_ge(degree_ready, s.i + 1)
                    wait_taken(pool, s.support)
                    d = d0[:, blocks].unsqueeze(2).broadcast_to([P, B, P])
                    nc.gpsimd.tensor_tensor(operand_of[L0][:, blocks, :], support0[:, blocks, :], d, ALU.mult)\
                        .then_inc(operand0_ready, 1)
                    if s.i:
                        pool.wait_ge(small_done, s.diag_free)
                    nc.gpsimd.tensor_tensor(diag[:, :, :], ident[:, :].unsqueeze(1).broadcast_to([P, B, P]), d,
                                            ALU.mult).then_inc(diag_ready, 1)
                elif s.kind == "layer3_degrees":
                    pool.wait_ge(degree3_in_ready, 1)
                    nc.gpsimd.tensor_tensor(d3[:, :], deg3_in[:, 0, :], minus_half[:, :], ALU.pow)\
                        .then_inc(degree3_raw, 1)
                elif s.kind == "batch_norm":
                    pool.wait_ge(bn_variance_ready, 1)
                    nc.gpsimd.tensor_tensor(bn_rstd[:, :], bn_var[:, :], minus_half[:, 0:1], ALU.pow)\
                        .then_inc(bn_rstd_ready, 1)
                elif s.kind == "radial_mask" and s.i == s.j:
                    pool.wait_ge(weights_masked, s.ready[1])
                    w = weights[:, s.n % S_SLOTS, :, :]
                    nc.gpsimd.affine_select(out=w, in_=w, compare_op=ALU.not_equal, fill=0.0, base=0,
                                            pattern=[[-P, B], [1, PANEL]], channel_multiplier=-1)\
                        .then_inc(diagonal_cleared, 1)

        @block.scalar
        def _(act):
            order = [0]

            def then(ins):
                order[0] += 1
                ins.then_inc(act_order, 1)
                act.wait_ge(act_order, order[0])

            for to, frm in first_consts:
                act.dma_start(to, frm).then_inc(first_consts_loaded, 16)
            for to, frm in consts:
                act.dma_start(to, frm).then_inc(consts_loaded, 16)
            act.wait_ge(consts_made, CONSTS_MADE)
            silu_table = True
            for s in steps:
                if s.kind in ("transpose", "support", "degree_row") or s.kind == "dense" and s.layer != L3:
                    act.wait_ge(small_done, s.e + 1)
                blocks = slice(B * s.i, B * s.i + B)
                if s.kind == "chain_evacuate":
                    act.wait_ge(products_done, s.k + 1)
                    if s.main_count:
                        act.wait_ge(main_taken, s.main_count)
                    nc.scalar.activation(partial[:, s.i, :], banks["chain"][s.bank][:, :], ACT.Copy)\
                        .then_inc(chain_taken, 1)
                elif s.kind == "transpose":
                    if s.ht_free:
                        act.wait_ge(small_done, s.ht_free)
                    nc.scalar.activation(rows_t[:, s.ht % 2, :], small[s.bank][:, :], ACT.Copy)\
                        .then_inc(small_taken[s.bank], 1)
                elif s.kind == "support":
                    to = support0 if s.layer == IN else operand_of[L2]
                    nc.scalar.activation(to[:, blocks, :], by_block(small[s.bank][:, :]), ACT.Copy)\
                        .then_inc(small_taken[s.bank], 1)
                elif s.kind == "degree_row":
                    nc.scalar.activation(degree_rows[:, s.i, :], small[s.bank][:, :], ACT.Copy)\
                        .then_inc(small_taken[s.bank], 1)
                elif s.kind == "scale":
                    h = s.norm % 2
                    act.wait_ge(shift_ready, s.first_norms + 1)
                    if s.layer == IN and s.rows_free:
                        act.wait_ge(small_done, s.rows_free)
                    for b in range(B):
                        to = rows[:, s.rows % 2, b, :] if s.layer == IN else operand_of[L1A][:, B * s.i + b, :]
                        last = nc.scalar.activation(to, x[:, B * s.i + b, :], ACT.Relu, scale=ln_rstd[:, h, b:b + 1],
                                                    bias=ln_shift[:, h, b:b + 1])
                    last.then_inc(normed, 1)
                elif s.kind == "bn_apply":
                    act.wait_ge(bn_affine_ready, 1)
                    if s.ev_free:
                        act.wait_ge(small_done, s.ev_free)
                    nc.scalar.activation(sums_t[:, s.ev % 2, :], partial[:, s.i, :], ACT.Relu,
                                         scale=bn_affine[:, 0:1], bias=bn_affine[:, 2:3]).then_inc(bn_applied, 1)
                elif s.kind == "dense" and s.layer == L1A:
                    silu_table = True
                    nc.scalar.activation(operand_of[L1B][:, blocks, :], by_block(small[s.bank][:, :]), ACT.Silu)\
                        .then_inc(small_taken[s.bank], 1)
                elif s.kind == "dense" and s.layer == L1B:
                    if s.silu_free:
                        act.wait_ge(normed, s.silu_free)
                    silu_table = True
                    nc.scalar.activation(silu[:, s.silu % 2, :, :], by_block(small[s.bank][:, :]), ACT.Silu)\
                        .then_inc(small_taken[s.bank], 1)
                elif s.kind == "dense" and s.layer == L3:
                    wait_taken(act, s.e)
                    act.dma_start(out[PANEL * s.i:PANEL * s.i + PANEL, :].rearrange("(b p) f -> p b f", p=P),
                                  scratch[:, s.result % 2, :, :]).then_inc(stored[s.result % 2], 16)
                elif s.kind == "radial_seed":
                    y = recips[:, s.m % Y_SLOTS, :, :]
                    wait_loaded(act, s.visit)
                    if s.m >= Y_SLOTS:
                        act.wait_ge(weights_masked, s.m - Y_SLOTS + 1)
                    if s.m == 0:
                        act.wait_ge(radial_ready, 1)
                    if silu_table:
                        nc.scalar.preload_act_table_set("natural_log_exp_and_others")
                        silu_table = False
                    then(nc.scalar.activation(y, tiles[:, s.visit % TILE_SLOTS, :, :], ACT.Ln, bias=tiny[:, 0:1]))
                    nc.scalar.activation(y, y, ACT.Exp, scale=-1.0).then_inc(recip_seeded, 1)
                elif s.kind == "radial_exp":
                    y = recips[:, s.m % Y_SLOTS, :, :]
                    if silu_table:
                        nc.scalar.preload_act_table_set("natural_log_exp_and_others")
                        silu_table = False
                    act.wait_ge(recip_done, s.m + 1)
                    then(nc.scalar.activation(y, y, ACT.Square, bias=radial[:, 2:3]))
                    nc.scalar.activation(y, y, ACT.Exp, scale=radial[:, 5:6]).then_inc(exp_done, 1)
                elif s.kind == "radial_store":
                    wait_weights(act, s.ready)
                    act.dma_start(kept[s.i, s.j, :, :, :], weights[:, s.n % S_SLOTS, :, :])\
                        .then_inc(weights_stored[s.n % S_SLOTS], 16)
            act.wait_ge(stored[0], 16 * (NP // 2))
            act.wait_ge(stored[1], 16 * (NP // 2))

        @block.vector
        def _(dve):
            order = [0]

            def then(ins):
                order[0] += 1
                ins.then_inc(dve_order, 1)
                dve.wait_ge(dve_order, order[0])

            def over_blocks(ap):
                return ap.unsqueeze(2).broadcast_to([P, B, P])

            def layer_norm(s, to):
                h = s.norm % 2
                xs = x[:, B * s.i:B * s.i + B, :]
                for b in range(B):
                    last = nc.vector.bn_stats(ln_stats[:, b, :], xs[:, b, :])
                then(last)
                for b in range(B):
                    last = nc.vector.bn_aggr(ln_mv[:, b, :], ln_stats[:, b, :])
                then(last)
                if s.layer in (IN, "batch_norm"):
                    if s.norm >= 2:
                        dve.wait_ge(normed, s.norm - 1)
                    then(nc.vector.tensor_scalar(ln_negmean[:, h, :], ln_mv[:, :, 0], -1.0, None, ALU.mult))
                    nc.vector.tensor_scalar(ln_var[:, h, :], ln_mv[:, :, 1], LN_EPS, None, ALU.add)\
                        .then_inc(variance_ready, 1)
                    return
                nc.vector.tensor_scalar(ln_var[:, h, :], ln_mv[:, :, 1], LN_EPS, None, ALU.add)\
                    .then_inc(variance_ready, 1)
                then(nc.vector.tensor_tensor(scratch[:, h, :, :], xs, over_blocks(ln_mv[:, :, 0]), ALU.subtract))
                dve.wait_ge(rstd_ready, s.norm + 1)
                scale = ln_rstd[:, h, :]
                if s.layer == L2:
                    then(nc.vector.tensor_tensor(ln_scale[:, :], scale, d3[:, B * s.i:B * s.i + B], ALU.mult))
                    scale = ln_scale[:, :]
                nc.vector.scalar_tensor_tensor(out=to, in0=scratch[:, h, :, :], scalar=0.0, in1=over_blocks(scale),
                                               op0=ALU.max, op1=ALU.mult).then_inc(normed, 1)

            dve.wait_ge(x_loaded[0], 16)
            dve.wait_ge(consts_made, CONSTS_MADE)
            for s in steps:
                blocks = slice(B * s.i, B * s.i + B)
                if s.kind == "row_add":
                    acc = row_acc[:, s.i % 2, :, :]
                    wait_loaded(dve, s.visit)
                    tile = tiles[:, s.visit % TILE_SLOTS, :, :]
                    if s.n == 1:
                        if s.i >= 2:
                            dve.wait_ge(small_done, s.acc_free)
                        before = tiles[:, (s.visit - 1) % TILE_SLOTS, :, :]
                        nc.vector.tensor_tensor(acc, before, tile, ALU.add).then_inc(rows_added, 2)
                    elif s.n:
                        dve.wait_ge(rows_added, s.visit)
                        nc.vector.tensor_tensor(acc, acc, tile, ALU.add).then_inc(rows_added, 1)
                    if s.last:
                        dve.wait_ge(rows_added, s.visit + 1)
                        then(nc.vector.tensor_tensor(acc[:, 0:2, :], acc[:, 0:2, :], acc[:, 2:4, :], ALU.add))
                        nc.vector.tensor_tensor(acc[:, 0, :], acc[:, 0, :], acc[:, 1, :], ALU.add)\
                            .then_inc(blocks_added, 1)
                elif s.kind == "fold":
                    dve.wait_ge(small_done, s.e + 1)
                    sums = small[s.bank][:, 0:B]
                    nc.vector.tensor_copy(row_sum[:, blocks], sums)
                    nc.vector.tensor_scalar(deg_in[:, blocks], sums, DEG_EPS, None, ALU.add)\
                        .then_inc(small_taken[s.bank], 1)
                elif s.kind == "layer3_degrees":
                    wait_taken(dve, s.e)
                    then(nc.vector.tensor_scalar(deg3_in[:, 0, :], row_sum[:, :], 1.0, None, ALU.add))
                    then(nc.vector.tensor_scalar(deg3_in[:, 1, :], deg3_in[:, 0, :], 0.0, None, ALU.is_gt))
                    nc.vector.tensor_scalar(deg3_in[:, 0, :], deg3_in[:, 0, :], 1e-30, None, ALU.max)\
                        .then_inc(degree3_in_ready, 1)
                    dve.wait_ge(degree3_raw, 1)
                    then(nc.vector.tensor_tensor(d3[:, :], d3[:, :], deg3_in[:, 1, :], ALU.mult))
                elif s.kind == "layer0_evacuate":
                    part = partial[:, s.i, :]
                    dve.wait_ge(chain_taken, s.chain_count)
                    if s.k is not None:
                        dve.wait_ge(products_done, s.k + 1)
                        nc.vector.tensor_tensor(part, banks["main"][s.bank][:, :], part, ALU.add)\
                            .then_inc(main_taken, 1)
                        dve.wait_ge(main_taken, s.i + 1)
                    wait_taken(dve, s.e)
                    then(nc.vector.tensor_tensor(part, part, degree_rows[:, s.i, :], ALU.mult))
                    nc.vector.bn_stats(bn_stats[:, s.i, :], part).then_inc(layer0_out, 1)
                elif s.kind == "batch_norm":
                    dve.wait_ge(layer0_out, NP)
                    then(nc.vector.bn_aggr(bn_mv[:, :], bn_stats[:, :, :].rearrange("p n s -> p (n s)")))
                    nc.vector.tensor_scalar(bn_var[:, :], bn_mv[:, 1:2], BN_EPS, None, ALU.add)\
                        .then_inc(bn_variance_ready, 1)
                    dve.wait_ge(bn_rstd_ready, 1)
                    dve.wait_ge(consts_loaded, CONSTS_LOADED)
                    then(nc.vector.tensor_tensor(bn_affine[:, 0:1], bn_rstd[:, :], col_vec[:, 0:1], ALU.mult))
                    then(nc.vector.tensor_tensor(bn_affine[:, 1:2], bn_mv[:, 0:1], bn_affine[:, 0:1], ALU.mult))
                    nc.vector.tensor_tensor(bn_affine[:, 2:3], col_vec[:, 1:2], bn_affine[:, 1:2], ALU.subtract)\
                        .then_inc(bn_affine_ready, 1)
                    dve.wait_ge(small_done, s.e + 1)
                    then(nc.vector.tensor_copy(radial[:, 0:2], small[s.bank][:, P:P + 2]))
                    then(nc.vector.reciprocal(radial[:, 2:3], radial[:, 0:1]))
                    then(nc.vector.tensor_scalar(radial[:, 3:4], radial[:, 1:2], radial[:, 1:2], -2.0, ALU.mult, ALU.mult))
                    then(nc.vector.reciprocal(radial[:, 5:6], radial[:, 3:4]))
                    nc.vector.tensor_copy(radial[:, 4:5], radial[:, 5:6]).then_inc(radial_ready, 1)
                    nc.vector.tensor_copy(bias3[:, :], small[s.bank][:, 0:P]).then_inc(small_taken[s.bank], 1)
                elif s.kind == "main_evacuate":
                    dve.wait_ge(products_done, s.k + 1)
                    if s.ev_free:
                        dve.wait_ge(small_done, s.ev_free)
                    to = sums_t[:, s.ev % 2, :]
                    if s.chain_count:
                        dve.wait_ge(chain_taken, s.chain_count)
                        nc.vector.tensor_tensor(to, banks["main"][s.bank][:, :], partial[:, s.i, :], ALU.add)\
                            .then_inc(main_taken, 1)
                    else:
                        nc.vector.tensor_copy(to, banks["main"][s.bank][:, :]).then_inc(main_taken, 1)
                elif s.kind == "norm":
                    xs = x[:, blocks, :]
                    if s.norm == 2:
                        dve.wait_ge(x_loaded[1], 16)
                    if s.e is not None:
                        dve.wait_ge(small_done, s.e + 1)
                        nc.vector.tensor_tensor(xs, xs, by_block(small[s.e % SMALL_BANKS][:, :]), ALU.add)\
                            .then_inc(small_taken[s.e % SMALL_BANKS], 1)
                        wait_taken(dve, s.e)
                    if s.layer == L1B:
                        wait_taken(dve, s.silu_e)
                        then(nc.vector.tensor_tensor(xs, xs, silu[:, s.silu % 2, :, :], ALU.add))
                    if s.layer == L1B:
                        if s.rows_free:
                            dve.wait_ge(small_done, s.rows_free)
                        layer_norm(s, rows[:, s.rows % 2, :, :])
                    elif s.layer == L2:
                        layer_norm(s, operand_of[L3][:, blocks, :])
                    else:
                        layer_norm(s, None)
                elif s.kind == "dense" and s.layer == L3:
                    xs = x[:, blocks, :]
                    if s.result == 0:
                        wait_taken(dve, s.bias3)
                    then(nc.vector.tensor_tensor(xs, xs, bias3[:, :].unsqueeze(1).broadcast_to([P, B, P]), ALU.add))
                    dve.wait_ge(small_done, s.e + 1)
                    if s.result >= 2:
                        dve.wait_ge(stored[s.result % 2], 16 * (s.result // 2))
                    for b in range(B):
                        n = B * s.i + b
                        last = nc.vector.scalar_tensor_tensor(
                            out=scratch[:, s.result % 2, b, :], in0=small[s.bank][:, b * P:b * P + P],
                            scalar=d3[:, n:n + 1], in1=x[:, n, :], op0=ALU.mult, op1=ALU.add)
                    last.then_inc(small_taken[s.bank], 1)
                elif s.kind == "radial_newton":
                    y = recips[:, s.m % Y_SLOTS, :, :]
                    t = weights[:, s.n % S_SLOTS, :, :]
                    dve.wait_ge(recip_seeded, s.m + 1)
                    wait_slot_free(dve, s.free)
                    then(nc.vector.tensor_tensor(t, tiles[:, s.visit % TILE_SLOTS, :, :], y, ALU.mult))
                    flat = lambda a: a.rearrange("p b n -> p (b n)")
                    nc.vector.scalar_tensor_tensor(out=flat(y), in0=flat(t), scalar=2.0, in1=flat(y),
                                                   op0=ALU.subtract, op1=ALU.mult).then_inc(recip_done, 1)
                elif s.kind == "radial_mask":
                    dve.wait_ge(exp_done, s.m + 1)
                    nc.vector.scalar_tensor_tensor(
                        out=weights[:, s.n % S_SLOTS, :, :], in0=tiles[:, s.visit % TILE_SLOTS, :, :], scalar=CUTOFF,
                        in1=recips[:, s.m % Y_SLOTS, :, :], op0=ALU.is_lt, op1=ALU.mult).then_inc(weights_masked, 1)

        @block.tensor
        def _(pe):
            def wait_operand(made_by):
                what, n = made_by
                if what == "small":
                    wait_taken(pe, n)
                elif what == "norm":
                    pe.wait_ge(normed, n + 1)
                elif what == "pool":
                    pe.wait_ge(operand0_ready, n + 1)

            def wait_sums(ready):
                what, n = ready
                if what == "main":
                    pe.wait_ge(main_taken, n + 1)
                else:
                    pe.wait_ge(bn_applied, n)

            pe.wait_ge(consts_made, CONSTS_MADE)
            pe.wait_ge(first_consts_loaded, 32)
            for s in steps:
                if s.bank_uses:
                    pe.wait_ge(small_taken[s.bank], s.bank_uses)
                if s.kind == "product":
                    if s.layer == L2:
                        wait_weights(pe, s.ready)
                        moving = weights[:, s.n % S_SLOTS, :, :]
                    else:
                        wait_loaded(pe, s.visit)
                        moving = tiles[:, s.visit % TILE_SLOTS, :, :]
                    wait_operand(s.operand)
                    if s.first and s.bank_free:
                        pe.wait_ge(main_taken if s.group == "main" else chain_taken, s.bank_free)
                    bank = banks[s.group][s.bank]
                    for b in range(B):
                        last = nc.tensor.matmul(bank[:, :], operand_of[s.layer][:, B * s.j + b, :], moving[:, b, :],
                                                start=s.first and b == 0, stop=s.last and b == B - 1)
                        if s.layer == L3 and s.i == s.j and b == 0:
                            for c in range(B):
                                nc.tensor.matmul(bank[:, c * P:c * P + P], operand_of[L3][:, B * s.j + c, :],
                                                 ident[:, :], start=False, stop=False)
                    last.then_inc(products_done, 1)
                elif s.kind == "dense":
                    wait_sums(s.ready)
                    for b in range(B):
                        to = small[s.bank][:, b * P:b * P + P]
                        last = nc.tensor.matmul(to, sums_t[:, s.ev % 2, b * P:b * P + P],
                                                w_sb[:, 3 if s.layer == L3 else 1, :], start=True, stop=s.layer == L3)
                        if s.layer != L3:
                            last = nc.tensor.matmul(to, ones[0:1, :], row_vec[0:1, 1, :], start=False, stop=True)
                    last.then_inc(small_done, 1)
                elif s.kind == "untranspose":
                    wait_sums(s.ready)
                    for b in range(B):
                        last = nc.tensor.transpose(small[s.bank][:, b * P:b * P + P],
                                                   sums_t[:, s.ev % 2, b * P:b * P + P], ident[:, :])
                    last.then_inc(small_done, 1)
                elif s.kind == "transpose":
                    pe.wait_ge(normed, s.norm + 1)
                    for b in range(B):
                        last = nc.tensor.transpose(small[s.bank][:, b * P:b * P + P], rows[:, s.rows % 2, b, :],
                                                   ident[:, :])
                    last.then_inc(small_done, 1)
                elif s.kind == "support":
                    wait_taken(pe, s.ht_e)
                    w = 0 if s.layer == IN else 2
                    for b in range(B):
                        to = small[s.bank][:, b * P:b * P + P]
                        nc.tensor.matmul(to, rows_t[:, s.ht % 2, b * P:b * P + P], w_sb[:, w, :],
                                         start=True, stop=False)
                        last = nc.tensor.matmul(to, ones[0:1, :], row_vec[0:1, w, :], start=False, stop=True)
                    last.then_inc(small_done, 1)
                elif s.kind == "fold":
                    pe.wait_ge(blocks_added, s.i + 1)
                    for b in range(B):
                        last = nc.tensor.matmul(small[s.bank][:, b:b + 1], row_acc[:, s.i % 2, 0, b * P:b * P + P],
                                                ones[:, 0:1], start=True, stop=True)
                    last.then_inc(small_done, 1)
                elif s.kind == "degree_row":
                    pe.wait_ge(diag_ready, s.i + 1)
                    nc.tensor.matmul(small[s.bank][:, :], ones[:, :], diag[:, :, :].rearrange("p b n -> p (b n)"),
                                     start=True, stop=True).then_inc(small_done, 1)
                elif s.kind == "batch_norm":
                    pe.wait_ge(consts_loaded, CONSTS_LOADED)
                    nc.tensor.matmul(small[s.bank][:, 0:P], ones[0:1, :], row_vec[0:1, 3, :], start=True, stop=True)
                    nc.tensor.matmul(small[s.bank][:, P:P + 2], ones[0:1, :], radial_in[0:1, :],
                                     start=True, stop=True).then_inc(small_done, 1)


_INS = ["x", "adj", "L0_gnn_W", "L0_gnn_b", "L0_gnn_gamma", "L0_gnn_beta", "L1_gnn_W", "L1_gnn_b", "L2_gnn_W",
        "L2_gnn_B", "L2_gnn_mu", "L2_gnn_sigma", "L3_gnn_weight", "L3_gnn_bias"]
_OUTS = [((4096, 128), "float32")]


def kernel(**inputs):
    import numpy as _np
    import concourse.bacc as _bacc
    from concourse import mybir as _mybir
    from concourse.bass_utils import run_bass_kernel_spmd as _run

    nc = _bacc.Bacc("TRN2", target_bir_lowering=False, num_devices=1)
    arrays, args = {}, []
    for name in _INS:
        a = _np.ascontiguousarray(inputs[name])
        if name == "adj":
            a = _np.ascontiguousarray(a.reshape(NP, PANEL, NP, B, P).transpose(0, 2, 4, 3, 1))
        if name == "x":
            a = _np.ascontiguousarray(a.reshape(NBLK, P, P).transpose(1, 0, 2))
        arrays[f"in_{name}_dram"] = a
        args.append(nc.dram_tensor(f"in_{name}_dram", a.shape, _mybir.dt.from_np(a.dtype), kind="ExternalInput").ap())
    for i, (shape, dtype) in enumerate(_OUTS):
        dt = _mybir.dt.from_np(_np.dtype(dtype))
        args.append(nc.dram_tensor(f"out_{i}_dram", shape, dt, kind="ExternalOutput").ap())
    graph_layers_kernel(nc, *args)
    r = _run(nc, [arrays], core_ids=[0])
    got = tuple(r.results[0][f"out_{i}_dram"] for i in range(len(_OUTS)))
    return got[0]
```

```python
import concourse.bass as bass
from concourse import mybir
from contextlib import ExitStack

P = 128
N = 4096
PANEL = 512
NP = N // PANEL
B = PANEL // P
NBLK = N // P
TILE_SLOTS = 9
S_SLOTS = 3
KEEP_AT, USE_AT = (0, 2, 3, 5), (-8, -6, -5, -4)
ONES_AHEAD = 2
KEPT_LOAD_AHEAD = 9
Y_SLOTS = 2
MAIN_BANKS, CHAIN_BANKS, SMALL_BANKS = 3, 2, 3
IN, L0, L1A, L1B, L2, L3 = "input", 0, 1, 2, 3, 4
LN_EPS = 1e-5
BN_EPS = 1e-5
DEG_EPS = 1e-6
TINY = 1e-18
CUTOFF = 0.5
SUPPORTS_AT = (0, 0, 11, 12, 25, 34, 39, 46)
BIAS_PARTS = 3
KEPT = ("x..x..x.",
        "x...x...",
        "xxx.x...",
        "xxx..x..",
        ".x.x.xx.",
        "xx...xxx",
        "x..xx..x",
        "x..x...x")
HOLD = 7
LONG_HOLD = 16
X_REST_AT = 11


def kept_in_dram(i, j):
    return KEPT[i][j] == "x"


def early_layer0(i, j):
    return j == i + 1 and i < 3


STAGES = {
    IN: [(0, "norm"), (1, "scale"), (3, "transpose"), (4, "support")],
    "degree": [(0, "fold"), (5, "degree_row")],
    "batch_norm": [(0, "bn_apply"), (2, "untranspose"), (2, "norm"), (3, "scale")],
    L1A: [(2, "dense")],
    L1B: [(1, "dense"), (2, "norm"), (4, "transpose"), (6, "support")],
    L2: [(1, "untranspose"), (2, "norm")],
    L3: [(2, "dense")],
}
MAKES = {("degree", "fold"): (L0, 3), ("batch_norm", "scale"): (L1A, 2), (L1A, "dense"): (L1B, 2),
         (L1B, "support"): (L2, 2), (L2, "norm"): (L3, 1)}


def sweeps():
    up = range(NP)
    fresh_last = lambda i, rest: [*range(i - 1), *rest, *range(max(i - 1, 0), i)]
    rows = [(i, j, False, j <= i or early_layer0(i, j)) for i in up for j in fresh_last(i, range(NP - 1, i, -1)) + [i]]
    l0 = [(i, j, True, False) for i in up for j in range(i + 1, NP) if not early_layer0(i, j)]
    l1a = [(i, j, True, False) for j in up for i in (0, 1)] + [(1, 0, False, True)]
    l1a += [(i, j, True, j < i) for i in range(2, NP) for j in fresh_last(i, range(i, NP))]
    turn = [(1, 1), (2, 2), (0, 0), (1, 0), (2, 1), (2, 0)]
    turn += [(i, j) for i in range(3, NP) for j in fresh_last(i, [i])]
    l1b = [(NP - 1 - i, NP - 1 - j, True, j < i) for i, j in turn]
    l2 = [(i, j, True, j < i) for i, j in turn]
    l3 = [(i, j, True, False) for i in up for j in range(i, NP)]
    return [(None, L0, rows), (L0, None, l0), (L1A, L1B, l1a), (L1B, L2, l1b), (L2, L3, l2), (L3, None, l3)]


class Step:

    def __init__(self, kind, layer=None, i=0, j=0, visit=None, k=None, e=None, bank=None, bank_uses=0, bank_free=None,
                 first=False, last=False, operand=None, products=0, ready=None, stages=None,
                 norm=None, ev=None, ev_free=0, rows=None, rows_free=0, ht=None, ht_free=0, ht_e=None,
                 support=None, diag_free=0, acc_free=0, chain_count=0, main_count=0, n=None):
        self.kind, self.layer = kind, layer
        self.i, self.j, self.visit = i, j, visit
        self.k = k
        self.e, self.bank, self.bank_uses = e, bank, bank_uses
        self.bank_free = bank_free
        self.first, self.last = first, last
        self.operand, self.ready = operand, ready
        self.products, self.stages = products, stages
        self.norm = norm
        self.ev, self.ev_free = ev, ev_free
        self.rows, self.rows_free = rows, rows_free
        self.ht, self.ht_free, self.ht_e = ht, ht_free, ht_e
        self.support = support
        self.diag_free, self.acc_free = diag_free, acc_free
        self.chain_count, self.main_count = chain_count, main_count
        self.n = n


class Planner:
    def __init__(self):
        self.steps, self.visits = [], []
        self.tick = 0
        self.count = dict.fromkeys(["product", "main", "chain", "small", "norm", "first_norms", "result"], 0)
        self.readers = {"ev": [], "rows": [], "ht": []}
        self.open = []
        self.late = []
        self.made_by, self.due, self.made = {}, {}, {}
        self.silu_norms = []
        self.summing_rows = False
        self.groups, self.bank_user = {}, {}
        self.size = {}

    def emit(self, kind, **fields):
        self.steps.append(Step(kind, **fields))
        return self.steps[-1]

    def small(self, kind, **fields):
        e = self.count["small"]
        self.count["small"] += 1
        return self.emit(kind, e=e, bank=e % SMALL_BANKS, bank_uses=e // SMALL_BANKS, **fields)

    def take(self, buffer):
        readers = self.readers[buffer]
        readers.append(None)
        n = len(readers) - 1
        return {buffer: n, buffer + "_free": readers[n - 2] + 1 if n >= 2 else 0}

    def stage(self, panel):
        _, what = panel.stages.pop(0)
        layer, i = panel.layer, panel.i
        if what == "dense":
            s = self.small("dense", layer=layer, i=i, ev=panel.ev, ready=panel.ready)
            self.readers["ev"][panel.ev] = s.e
            made_by = ("small", s.e)
            if layer == L1B:
                panel.silu = s.silu = len(self.silu_norms)
                panel.silu_e = s.e
                s.silu_free = self.silu_norms[s.silu - 2] + 1 if s.silu >= 2 else 0
                self.silu_norms.append(None)
            if layer == L3:
                s.result, s.bias3 = self.count["result"], self.made["bias3"]
                self.count["result"] += 1
        elif what == "untranspose":
            panel.e = self.small("untranspose", layer=layer, i=i, ev=panel.ev, ready=panel.ready).e
            self.readers["ev"][panel.ev] = panel.e
        elif what == "bn_apply":
            ev = self.take("ev")
            panel.ev, panel.ready = ev["ev"], ("bn_applied", i + 1)
            self.emit("bn_apply", i=i, **ev)
        elif what == "norm":
            s = self.emit("norm", layer=layer, i=i, norm=self.count["norm"], rows=None, e=None)
            self.count["norm"] += 1
            if layer == L1B:
                half = self.take("rows")
                panel.rows, s.rows, s.rows_free = half["rows"], half["rows"], half["rows_free"]
            if layer in ("batch_norm", L2):
                s.e = panel.e
            if layer == L1B:
                s.silu, s.silu_e = panel.silu, panel.silu_e
                self.silu_norms[s.silu] = s.norm
            panel.norm = s.norm
            made_by = ("norm", s.norm)
        elif what == "scale":
            s = self.emit("scale", layer=layer, i=i, norm=panel.norm)
            s.first_norms = self.count["first_norms"]
            self.count["first_norms"] += 1
            if layer == IN:
                half = self.take("rows")
                panel.rows, s.rows, s.rows_free = half["rows"], half["rows"], half["rows_free"]
            made_by = ("norm", panel.norm)
        elif what == "transpose":
            s = self.small("transpose", layer=layer, i=i, rows=panel.rows, norm=panel.norm, **self.take("ht"))
            self.readers["rows"][panel.rows] = s.e
            panel.ht, panel.ht_e = s.ht, s.e
        elif what == "support":
            s = self.small("support", layer=layer, i=i, ht=panel.ht, ht_e=panel.ht_e)
            self.readers["ht"][panel.ht] = s.e
            made_by = ("small", s.e)
            if layer == IN:
                self.made["support", i] = s.e
        elif what == "fold":
            self.made["fold", i] = self.small("fold", i=i, support=self.made["support", i],
                                              diag_free=self.made.get(("degree_row", i - 1), -1) + 1).e
            made_by = ("pool", i)
        elif what == "degree_row":
            panel.e = self.small("degree_row", i=i).e
            self.made["degree_row", i] = panel.e
        if (layer, what) in MAKES:
            of, time = MAKES[layer, what]
            self.made_by[of, i] = made_by
            self.due[of, i] = self.tick + time

    def begin(self, layer, i, start, **fields):
        panel = Step("panel", layer=layer, i=i, stages=[(start + d, w) for d, w in STAGES[layer]], **fields)
        self.open.append(panel)
        return panel

    def run_due(self):
        for panel in self.open:
            while panel.stages and panel.stages[0][0] <= self.tick:
                self.stage(panel)
        self.open = [p for p in self.open if p.stages]
        ready = [t for t in self.late if self.due.get((t[1], t[3]), 1 << 30) <= self.tick]
        kept = [t for t in self.late if t[0] <= len(self.visits) - (LONG_HOLD if t[3] > t[2] and t[1] == L0 else HOLD)]
        if kept or ready:
            for t in ready + [t for t in kept if t not in ready]:
                self.late.remove(t)
                self.product(*t, "chain")
            self.run_due()

    def take_until(self, made, what):
        while what not in made:
            self.stage(next(panel for panel in self.open if panel.stages))

    def need(self, layer, j):
        self.take_until(self.made_by, (layer, j))

    def product(self, v, layer, i, j, kind):
        self.need(layer, j)
        key = (kind, layer, i)
        if key not in self.groups:
            taken = [g.bank for g in self.groups.values()]
            free = [(kind, b) for b in range(MAIN_BANKS if kind == "main" else CHAIN_BANKS)]
            if kind == "chain" and layer == L0:
                free += [("main", MAIN_BANKS - 1)]
            free = [b for b in free if b not in taken]
            bank = min(free, key=lambda b: (b[0] != kind, self.bank_user.get(b, (kind, 0))[1]))
            self.groups[key] = Step("group", bank=bank, products=0, bank_free=self.bank_user.get(bank, (kind, 0)))
        g = self.groups[key]
        g.products += 1
        last = g.products == self.size[key]
        k = self.count["product"]
        self.emit("product", k=k, visit=v, layer=layer, i=i, j=j, bank=g.bank, first=g.products == 1,
                  last=last, bank_free=g.bank_free, operand=self.made_by[layer, j])
        self.count["product"] += 1
        self.tick += 1
        if not last:
            return
        del self.groups[key]
        n = self.count[kind]
        self.count[kind] += 1
        self.bank_user[g.bank] = (kind, n + 1)
        if kind == "chain":
            self.emit("chain_evacuate", layer=layer, i=i, bank=g.bank, k=k, main_count=self.count["main"])
            self.made["partial", layer, i] = n + 1
            if (layer, i) == (L0, NP - 1):
                self.take_until(self.made, ("degree_row", i))
                self.emit("layer0_evacuate", i=i, chain_count=n + 1, e=self.made["degree_row", i])
        elif layer == L0:
            self.take_until(self.made, ("degree_row", i))
            self.emit("layer0_evacuate", i=i, bank=g.bank, k=k, chain_count=self.made["partial", layer, i],
                      e=self.made["degree_row", i])
        else:
            ev = self.take("ev")
            self.emit("main_evacuate", layer=layer, i=i, bank=g.bank, k=k,
                      chain_count=self.made.get(("partial", layer, i), 0), **ev)
            self.begin(layer, i, self.tick, ready=("main", n), **ev)

    def radial_steps(self):
        products = [s for s in self.steps if s.kind == "product"]
        keeps = [s for s in products if s.layer == L1A and kept_in_dram(s.i, s.j)]
        uses = [s for s in products if s.layer == L2]
        at = {}
        seeds, masks, freed, before = [], [], [], 0
        counts = {"masked": 0, "cleared": 0}
        slot_loads, slot_stores = [0] * S_SLOTS, [0] * S_SLOTS
        stored = {}

        def place(k, order, step):
            at.setdefault(k, []).append((order, step))

        for n, s in enumerate(keeps + uses):
            keep, slot = s.layer == L1A, n % S_SLOTS
            fields = dict(n=n, visit=s.visit, i=s.i, j=s.j)
            free = freed[n - S_SLOTS] if n >= S_SLOTS else (0, None)
            before = max(before, free[0])
            if keep or not kept_in_dram(s.i, s.j):
                m = len(masks)
                ahead = KEEP_AT if keep else USE_AT
                seed = max(s.k + ahead[0], masks[m - Y_SLOTS] if m >= Y_SLOTS else 0, seeds[-1] if seeds else 0)
                newton = max(s.k + ahead[1], seed + 1, before)
                exp = max(s.k + ahead[2], newton + 1)
                mask = max(s.k + ahead[3], exp + 1)
                seeds.append(seed)
                masks.append(mask)
                before = newton
                counts["masked"] += 1
                counts["cleared"] += s.i == s.j
                ready = ("masked", counts["masked"], counts["cleared"] if s.i == s.j else 0)
                for kind, k, order in (("radial_seed", seed, n), ("radial_newton", newton, n + 0.1),
                                       ("radial_exp", exp, n + 1.4), ("radial_mask", mask, n + 1.5)):
                    step = Step(kind, **fields)
                    step.m, step.free, step.ready = m, free[1], ready
                    place(k, order, step)
                if keep:
                    slot_stores[slot] += 1
                    step = Step("radial_store", **fields)
                    step.ready = ready
                    place(mask + 1, n + 1.7, step)
                    stored[s.i, s.j] = (slot, slot_stores[slot])
                    freed.append((mask + 1, ("stored", slot, slot_stores[slot])))
            else:
                slot_loads[slot] += 1
                before = max(before, s.k - KEPT_LOAD_AHEAD)
                step = Step("radial_load", **fields)
                step.free, step.stored = free[1], stored[s.i, s.j]
                place(before, n, step)
                ready = ("loaded", slot, slot_loads[slot])
            if not keep:
                s.n, s.ready = n, ready
                freed.append((s.k, ("used", s.k + 1)))
        for n, s in enumerate(s for s in products if s.layer == L3 and s.i == s.j):
            s.ones = n + 1
            place(s.k - ONES_AHEAD, -1, Step("add_ones", visit=s.visit, i=s.i, j=s.j))
        steps, due = [], []
        for s in self.steps:
            if s.kind == "product":
                steps += due
                due = [step for _, step in sorted(at.get(s.k, []), key=lambda t: t[0])]
            steps.append(s)
        self.steps = steps + due

    def tile_loads(self):
        first, last = {}, {}
        for v in self.visits:
            v.k = v.radial = v.added = 0
        for t, s in enumerate(self.steps):
            uses_tile = s.kind in ("row_add", "radial_seed", "radial_newton", "radial_mask", "add_ones") or s.kind == "product" and s.layer != L2
            if not uses_tile:
                continue
            v = self.visits[s.visit]
            if s.kind == "product":
                v.k = s.k + 1
            elif s.kind == "row_add":
                v.added = s.visit + (1 if s.n else 2)
                if s.n == 1:
                    last[s.visit - 1] = t
            elif s.kind == "radial_mask":
                v.radial = s.ready[1]
            first.setdefault(s.visit, t)
            last[s.visit] = t
        loads, at = {}, -1
        in_slot, turns = [None] * (TILE_SLOTS + 1), [0] * (TILE_SLOTS + 1)
        for v, visit in enumerate(self.visits):
            if v not in first:
                continue
            slots = range(TILE_SLOTS + (v < self.layer0_visits))
            slot = min(slots, key=lambda n: -1 if in_slot[n] is None else last[in_slot[n]])
            visit.slot, visit.before = slot, in_slot[slot]
            turns[slot] += 1
            visit.turn = turns[slot]
            if visit.before is not None:
                at = max(at, last[visit.before])
                assert at < first[v], ("a tile is kept too long", v)
            in_slot[slot] = v
            loads.setdefault(at, []).append(v)
        steps = [Step("load", visit=v) for v in loads.get(-1, [])]
        for t, s in enumerate(self.steps):
            steps.append(s)
            steps += [Step("load", visit=v) for v in loads.get(t, [])]
        self.steps = steps

    def run(self):
        all_sweeps = sweeps()
        for main, chain, tiles in all_sweeps:
            for i, _, m, ch in tiles:
                for key, on in ((("main", main, i), m), (("chain", chain, i), ch)):
                    self.size[key] = self.size.get(key, 0) + on
        for n, (main, chain, tiles) in enumerate(all_sweeps):
            if main == L1A:
                self.layer0_visits = len(self.visits)
            if chain == L0:
                for i in range(NP):
                    self.begin(IN, i, SUPPORTS_AT[i])
            if main == L1A:
                self.made["bias3"] = self.small("batch_norm").e
                for i in range(NP):
                    self.begin("batch_norm", i, self.tick + i)
                while (L1A, 0) not in self.made_by:
                    self.run_due()
                    self.tick += 1
            self.summing_rows = chain == L0
            self.run_due()
            for i, j, m, ch in tiles:
                if (main, i, j) == (L0, 2, NP - 1):
                    self.emit("layer3_degrees", e=self.made["fold", NP - 1])
                v = len(self.visits)
                self.visits.append(Step("visit", i=i, j=j))
                if chain == L0:
                    self.emit("row_add", visit=v, i=i, n=v % NP, last=v % NP == NP - 1,
                              acc_free=self.made.get(("fold", i - 2), -1) + 1)
                    if j == i:
                        self.begin("degree", i, self.tick)
                if m:
                    self.product(v, main, i, j, "main")
                if ch:
                    if self.due.get((chain, j), 1 << 30) <= self.tick and not self.summing_rows:
                        self.product(v, chain, i, j, "chain")
                    else:
                        self.late.append((v, chain, i, j))
                if chain == L0:
                    self.tick += 1
                self.run_due()
        while self.open or self.late:
            self.tick += 1
            self.run_due()
        self.radial_steps()
        self.tile_loads()
        return self.steps, self.visits


def graph_layers_kernel(nc, x_in, adj_in, w0, b0, gamma, beta, w1, b1, w2, b2, mu, sigma, w3, b3, out):
    fp32, bf16 = mybir.dt.float32, mybir.dt.bfloat16
    ACT = mybir.ActivationFunctionType
    ALU = mybir.AluOpType
    steps, visits = Planner().run()

    with ExitStack() as ctx:
        def sb(name, shape):
            return ctx.enter_context(nc.sbuf_tensor(name, shape, fp32))

        def sem(name):
            return ctx.enter_context(nc.semaphore(name))

        kept = nc.dram_tensor("kept_weights", [NP, NP, P, B, PANEL], fp32, kind="Internal").ap()
        tiles = sb("tiles", [P, TILE_SLOTS, B, PANEL])
        weights = sb("weights", [P, S_SLOTS, B, PANEL])
        recips = sb("recips", [P, Y_SLOTS, B, PANEL])
        x = sb("x", [P, NBLK, P])
        operands = [sb("operand_a", [P, NBLK, P]), sb("operand_b", [P, NBLK, P])]
        partial = sb("partial", [P, NP, PANEL])
        row_acc = recips
        degree_rows = weights[:, 0:2].rearrange("p s b n -> p (s b) n")
        operand_of = {L0: operands[1], L1A: operands[0], L1B: operands[1], L2: operands[0], L3: operands[1]}
        support0 = operands[0]
        sums_t = sb("sums_t", [P, 2, PANEL])
        rows = sb("rows", [P, 2, B, P])
        rows_t = sb("rows_t", [P, 2, PANEL])
        silu = sb("silu", [P, 2, B, P])
        scratch = sb("scratch", [P, 2, B, P])
        diag = sb("diag", [P, B, P])
        w_sb = sb("w_sb", [P, 4, P])
        biases = sb("biases", [BIAS_PARTS, 4, P])
        bias_rest = sb("bias_rest", [BIAS_PARTS, P])
        bias_sum = sb("bias_sum", [BIAS_PARTS, P])
        bias_part = ctx.enter_context(nc.sbuf_tensor("bias_part", [BIAS_PARTS, P], bf16))
        bias_parts = ctx.enter_context(nc.sbuf_tensor("bias_parts", [BIAS_PARTS, 3, P], bf16))
        bf16_ones = ctx.enter_context(nc.sbuf_tensor("bf16_ones", [BIAS_PARTS, P], bf16))
        col_vec = sb("col_vec", [P, 2])
        radial_in = sb("radial_in", [1, 2])
        radial = sb("radial", [P, 5])
        ident = sb("ident", [P, P])
        ones = sb("ones", [P, P])
        bias3 = sb("bias3", [P, P])
        tiny = sb("tiny", [P, 1])
        minus_half = sb("minus_half", [P, NBLK])
        row_sum = sb("row_sum", [P, NBLK])
        deg_in = sb("deg_in", [P, NBLK])
        d0 = sb("d0", [P, NBLK])
        deg3_in = sb("deg3_in", [P, 2, NBLK])
        d3 = sb("d3", [P, NBLK])
        ln_stats = sb("ln_stats", [P, B, 6])
        ln_mv = sb("ln_mv", [P, B, 2])
        ln_var = sb("ln_var", [P, 2, B])
        ln_negmean = sb("ln_negmean", [P, 2, B])
        ln_rstd = sb("ln_rstd", [P, 2, B])
        ln_scale = sb("ln_scale", [P, B])
        ln_shift = sb("ln_shift", [P, 2, B])
        bn_stats = sb("bn_stats", [P, NP, 6])
        bn_mv = sb("bn_mv", [P, 2])
        bn_var = sb("bn_var", [P, 1])
        bn_rstd = sb("bn_rstd", [P, 1])
        bn_affine = sb("bn_affine", [P, 3])

        def psum(name):
            return ctx.enter_context(nc.psum_tensor(name, [P, PANEL], fp32))

        banks = {("main", b): psum(f"main_{b}") for b in range(MAIN_BANKS)}
        banks.update({("chain", b): psum(f"chain_{b}") for b in range(CHAIN_BANKS)})
        small = [psum(f"small_{b}") for b in range(SMALL_BANKS)]

        def by_block(ap):
            return ap.rearrange("p (b n) -> p b n", b=B)

        tile_loaded = [sem(f"tile_loaded_{s}") for s in range(TILE_SLOTS + 1)]
        x_loaded = [sem("x_loaded_first"), sem("x_loaded_rest")]
        first_consts_loaded = sem("first_consts_loaded")
        consts_loaded = sem("consts_loaded")
        zeroed = sem("zeroed")
        consts_made = sem("consts_made")
        ones_added = sem("ones_added")
        bias_split = sem("bias_split")
        products_done = sem("products_done")
        small_done = sem("small_done")
        small_taken = [sem(f"small_taken_{b}") for b in range(SMALL_BANKS)]
        main_taken = sem("main_taken")
        chain_taken = sem("chain_taken")
        rows_added = sem("rows_added")
        blocks_added = sem("blocks_added")
        layer0_out = sem("layer0_out")
        bn_applied = sem("bn_applied")
        normed = sem("normed")
        variance_ready = sem("variance_ready")
        rstd_ready = sem("rstd_ready")
        shift_ready = sem("shift_ready")
        degree_ready = sem("degree_ready")
        operand0_ready = sem("operand0_ready")
        diag_ready = sem("diag_ready")
        degree3_in_ready = sem("degree3_in_ready")
        degree3_raw = sem("degree3_raw")
        bn_variance_ready = sem("bn_variance_ready")
        bn_rstd_ready = sem("bn_rstd_ready")
        bn_affine_ready = sem("bn_affine_ready")
        radial_ready = sem("radial_ready")
        recip_seeded = sem("recip_seeded")
        recip_done = sem("recip_done")
        exp_done = sem("exp_done")
        weights_masked = sem("weights_masked")
        diagonal_cleared = sem("diagonal_cleared")
        weights_stored = [sem(f"weights_stored_{s}") for s in range(S_SLOTS)]
        weights_loaded = [sem(f"weights_loaded_{s}") for s in range(S_SLOTS)]
        stored = [sem("stored_0"), sem("stored_1")]
        act_order = sem("act_order")
        dve_order = sem("dve_order")

        def thrice(v):
            return v.rearrange("(a n) -> a n", a=1).broadcast_to([BIAS_PARTS, P])

        first_consts = [(w_sb[:, 0, :], w0[:, :]), (biases[:, 0, :], thrice(b0))]
        consts = [(biases[:, n, :], thrice(v)) for n, v in ((1, b1), (2, b2), (3, b3))]
        consts += [(col_vec[:, n:n + 1], v.rearrange("(n a) -> n a", a=1)) for n, v in enumerate([gamma, beta])]
        consts += [(radial_in[0:1, n:n + 1], v.rearrange("(a n) -> a n", a=1)) for n, v in enumerate([mu, sigma])]
        consts += [(w_sb[:, n, :], w[:, :]) for n, w in ((1, w1), (2, w2), (3, w3))]
        CONSTS_LOADED = 16 * len(consts)
        CONSTS_MADE = 5

        def wait_loaded(engine, v):
            engine.wait_ge(tile_loaded[visits[v].slot], 16 * visits[v].turn)

        def tile_of(v):
            slot = visits[v].slot
            return tiles[:, slot, :, :] if slot < TILE_SLOTS else weights[:, S_SLOTS - 1, :, :]

        def wait_taken(engine, e):
            engine.wait_ge(small_taken[e % SMALL_BANKS], e // SMALL_BANKS + 1)

        def wait_slot_free(engine, free):
            if free is None:
                return
            if free[0] == "stored":
                engine.wait_ge(weights_stored[free[1]], 16 * free[2])
            else:
                engine.wait_ge(products_done, free[1])

        def wait_weights(engine, ready):
            if ready[0] == "loaded":
                engine.wait_ge(weights_loaded[ready[1]], 16 * ready[2])
            else:
                engine.wait_ge(weights_masked, ready[1])
                if ready[2]:
                    engine.wait_ge(diagonal_cleared, ready[2])

        block = ctx.enter_context(nc.Block())

        @block.sync
        def _(sp):
            sp.dma_start(x[:, 0:2 * B, :], x_in[:, 0:2 * B, :]).then_inc(x_loaded[0], 16)
            for s in steps:
                if s.kind == "load":
                    v = visits[s.visit]
                    if s.visit == X_REST_AT:
                        sp.dma_start(x[:, 2 * B:NBLK, :], x_in[:, 2 * B:NBLK, :]).then_inc(x_loaded[1], 16)
                    if v.before is not None:
                        old = visits[v.before]
                        if old.k:
                            sp.wait_ge(products_done, old.k)
                        if old.added:
                            sp.wait_ge(rows_added, old.added)
                        if old.radial:
                            sp.wait_ge(weights_masked, old.radial)
                    sp.dma_start(tile_of(s.visit), adj_in[v.i, v.j, :, :, :]).then_inc(tile_loaded[v.slot], 16)
                elif s.kind == "radial_load":
                    sp.wait_ge(weights_stored[s.stored[0]], 16 * s.stored[1])
                    wait_slot_free(sp, s.free)
                    sp.dma_start(weights[:, s.n % S_SLOTS, :, :], kept[s.i, s.j, :, :, :])\
                        .then_inc(weights_loaded[s.n % S_SLOTS], 16)

        @block.gpsimd
        def _(pool):
            nc.gpsimd.memset(ident[:, :], 0.0).then_inc(zeroed, 1)
            nc.gpsimd.memset(ones[:, :], 1.0).then_inc(consts_made, 1)
            nc.gpsimd.memset(bf16_ones[:, :], 1.0).then_inc(consts_made, 1)
            nc.gpsimd.memset(tiny[:, :], TINY).then_inc(consts_made, 1)
            nc.gpsimd.memset(minus_half[:, :], -0.5).then_inc(consts_made, 1)
            pool.wait_ge(zeroed, 1)
            nc.gpsimd.affine_select(out=ident[:, :], in_=ident[:, :], compare_op=ALU.not_equal, fill=1.0, base=0,
                                    pattern=[[-1, P]], channel_multiplier=1).then_inc(consts_made, 1)
            pool.wait_ge(consts_made, CONSTS_MADE)
            for s in steps:
                if s.kind == "norm":
                    h = s.norm % 2
                    pool.wait_ge(variance_ready, s.norm + 1)
                    nc.gpsimd.tensor_tensor(ln_rstd[:, h, :], ln_var[:, h, :], minus_half[:, 0:B], ALU.pow)\
                        .then_inc(rstd_ready, 1)
                    if s.layer in (IN, "batch_norm"):
                        pool.wait_ge(rstd_ready, s.norm + 1)
                        nc.gpsimd.tensor_tensor(ln_shift[:, h, :], ln_negmean[:, h, :], ln_rstd[:, h, :], ALU.mult)\
                            .then_inc(shift_ready, 1)
                elif s.kind == "fold":
                    blocks = slice(B * s.i, B * s.i + B)
                    wait_taken(pool, s.e)
                    nc.gpsimd.tensor_tensor(d0[:, blocks], deg_in[:, blocks], minus_half[:, 0:B], ALU.pow)\
                        .then_inc(degree_ready, 1)
                    pool.wait_ge(degree_ready, s.i + 1)
                    wait_taken(pool, s.support)
                    d = d0[:, blocks].unsqueeze(2).broadcast_to([P, B, P])
                    nc.gpsimd.tensor_tensor(operand_of[L0][:, blocks, :], support0[:, blocks, :], d, ALU.mult)\
                        .then_inc(operand0_ready, 1)
                    if s.i:
                        pool.wait_ge(small_done, s.diag_free)
                    nc.gpsimd.tensor_tensor(diag[:, :, :], ident[:, :].unsqueeze(1).broadcast_to([P, B, P]), d,
                                            ALU.mult).then_inc(diag_ready, 1)
                elif s.kind == "layer3_degrees":
                    pool.wait_ge(degree3_in_ready, 1)
                    nc.gpsimd.tensor_tensor(d3[:, :], deg3_in[:, 0, :], minus_half[:, :], ALU.pow)\
                        .then_inc(degree3_raw, 1)
                elif s.kind == "batch_norm":
                    pool.wait_ge(bn_variance_ready, 1)
                    nc.gpsimd.tensor_tensor(bn_rstd[:, :], bn_var[:, :], minus_half[:, 0:1], ALU.pow)\
                        .then_inc(bn_rstd_ready, 1)
                elif s.kind == "radial_mask" and s.i == s.j:
                    pool.wait_ge(weights_masked, s.ready[1])
                    w = weights[:, s.n % S_SLOTS, :, :]
                    nc.gpsimd.affine_select(out=w, in_=w, compare_op=ALU.not_equal, fill=0.0, base=0,
                                            pattern=[[-P, B], [1, PANEL]], channel_multiplier=-1)\
                        .then_inc(diagonal_cleared, 1)

        @block.scalar
        def _(act):
            order = [0]

            def then(ins):
                order[0] += 1
                ins.then_inc(act_order, 1)
                act.wait_ge(act_order, order[0])

            for to, frm in first_consts:
                act.dma_start(to, frm).then_inc(first_consts_loaded, 16)
            for to, frm in consts:
                act.dma_start(to, frm).then_inc(consts_loaded, 16)
            act.wait_ge(consts_made, CONSTS_MADE)
            silu_table = True
            for s in steps:
                if s.kind in ("transpose", "support", "degree_row") or s.kind == "dense" and s.layer != L3:
                    act.wait_ge(small_done, s.e + 1)
                blocks = slice(B * s.i, B * s.i + B)
                if s.kind == "chain_evacuate":
                    act.wait_ge(products_done, s.k + 1)
                    if s.main_count:
                        act.wait_ge(main_taken, s.main_count)
                    nc.scalar.activation(partial[:, s.i, :], banks[s.bank][:, :], ACT.Copy)\
                        .then_inc(chain_taken, 1)
                elif s.kind == "transpose":
                    if s.ht_free:
                        act.wait_ge(small_done, s.ht_free)
                    nc.scalar.activation(rows_t[:, s.ht % 2, :], small[s.bank][:, :], ACT.Copy)\
                        .then_inc(small_taken[s.bank], 1)
                elif s.kind == "support":
                    to = support0 if s.layer == IN else operand_of[L2]
                    nc.scalar.activation(to[:, blocks, :], by_block(small[s.bank][:, :]), ACT.Copy)\
                        .then_inc(small_taken[s.bank], 1)
                elif s.kind == "degree_row":
                    nc.scalar.activation(degree_rows[:, s.i, :], small[s.bank][:, :], ACT.Copy)\
                        .then_inc(small_taken[s.bank], 1)
                elif s.kind == "scale":
                    h = s.norm % 2
                    act.wait_ge(shift_ready, s.first_norms + 1)
                    if s.layer == IN and s.rows_free:
                        act.wait_ge(small_done, s.rows_free)
                    for b in range(B):
                        to = rows[:, s.rows % 2, b, :] if s.layer == IN else operand_of[L1A][:, B * s.i + b, :]
                        last = nc.scalar.activation(to, x[:, B * s.i + b, :], ACT.Relu, scale=ln_rstd[:, h, b:b + 1],
                                                    bias=ln_shift[:, h, b:b + 1])
                    last.then_inc(normed, 1)
                elif s.kind == "bn_apply":
                    act.wait_ge(bn_affine_ready, 1)
                    if s.ev_free:
                        act.wait_ge(small_done, s.ev_free)
                    nc.scalar.activation(sums_t[:, s.ev % 2, :], partial[:, s.i, :], ACT.Relu,
                                         scale=bn_affine[:, 0:1], bias=bn_affine[:, 2:3]).then_inc(bn_applied, 1)
                elif s.kind == "dense" and s.layer == L1A:
                    silu_table = True
                    nc.scalar.activation(operand_of[L1B][:, blocks, :], by_block(small[s.bank][:, :]), ACT.Silu)\
                        .then_inc(small_taken[s.bank], 1)
                elif s.kind == "dense" and s.layer == L1B:
                    if s.silu_free:
                        act.wait_ge(normed, s.silu_free)
                    silu_table = True
                    nc.scalar.activation(silu[:, s.silu % 2, :, :], by_block(small[s.bank][:, :]), ACT.Silu)\
                        .then_inc(small_taken[s.bank], 1)
                elif s.kind == "dense" and s.layer == L3:
                    wait_taken(act, s.e)
                    act.dma_start(out[PANEL * s.i:PANEL * s.i + PANEL, :].rearrange("(b p) f -> p b f", p=P),
                                  scratch[:, s.result % 2, :, :]).then_inc(stored[s.result % 2], 16)
                elif s.kind == "radial_seed":
                    y = recips[:, s.m % Y_SLOTS, :, :]
                    wait_loaded(act, s.visit)
                    if s.m >= Y_SLOTS:
                        act.wait_ge(weights_masked, s.m - Y_SLOTS + 1)
                    if s.m == 0:
                        act.wait_ge(radial_ready, 1)
                    if silu_table:
                        nc.scalar.preload_act_table_set("natural_log_exp_and_others")
                        silu_table = False
                    then(nc.scalar.activation(y, tile_of(s.visit), ACT.Ln, bias=tiny[:, 0:1]))
                    nc.scalar.activation(y, y, ACT.Exp, scale=-1.0).then_inc(recip_seeded, 1)
                elif s.kind == "radial_exp":
                    y = recips[:, s.m % Y_SLOTS, :, :]
                    if silu_table:
                        nc.scalar.preload_act_table_set("natural_log_exp_and_others")
                        silu_table = False
                    act.wait_ge(recip_done, s.m + 1)
                    then(nc.scalar.activation(y, y, ACT.Square, bias=radial[:, 2:3]))
                    nc.scalar.activation(y, y, ACT.Exp, scale=radial[:, 4:5]).then_inc(exp_done, 1)
                elif s.kind == "radial_store":
                    wait_weights(act, s.ready)
                    act.dma_start(kept[s.i, s.j, :, :, :], weights[:, s.n % S_SLOTS, :, :])\
                        .then_inc(weights_stored[s.n % S_SLOTS], 16)
            act.wait_ge(stored[0], 16 * (NP // 2))
            act.wait_ge(stored[1], 16 * (NP // 2))

        @block.vector
        def _(dve):
            order = [0]

            def then(ins):
                order[0] += 1
                ins.then_inc(dve_order, 1)
                dve.wait_ge(dve_order, order[0])

            def over_blocks(ap):
                return ap.unsqueeze(2).broadcast_to([P, B, P])

            def layer_norm(s, to):
                h = s.norm % 2
                xs = x[:, B * s.i:B * s.i + B, :]
                for b in range(B):
                    last = nc.vector.bn_stats(ln_stats[:, b, :], xs[:, b, :])
                then(last)
                for b in range(B):
                    last = nc.vector.bn_aggr(ln_mv[:, b, :], ln_stats[:, b, :])
                then(last)
                if s.layer in (IN, "batch_norm"):
                    if s.norm >= 2:
                        dve.wait_ge(normed, s.norm - 1)
                    then(nc.vector.tensor_scalar(ln_negmean[:, h, :], ln_mv[:, :, 0], -1.0, None, ALU.mult))
                    nc.vector.tensor_scalar(ln_var[:, h, :], ln_mv[:, :, 1], LN_EPS, None, ALU.add)\
                        .then_inc(variance_ready, 1)
                    return
                nc.vector.tensor_scalar(ln_var[:, h, :], ln_mv[:, :, 1], LN_EPS, None, ALU.add)\
                    .then_inc(variance_ready, 1)
                then(nc.vector.tensor_tensor(scratch[:, h, :, :], xs, over_blocks(ln_mv[:, :, 0]), ALU.subtract))
                dve.wait_ge(rstd_ready, s.norm + 1)
                scale = ln_rstd[:, h, :]
                if s.layer == L2:
                    then(nc.vector.tensor_tensor(ln_scale[:, :], scale, d3[:, B * s.i:B * s.i + B], ALU.mult))
                    scale = ln_scale[:, :]
                nc.vector.scalar_tensor_tensor(out=to, in0=scratch[:, h, :, :], scalar=0.0, in1=over_blocks(scale),
                                               op0=ALU.max, op1=ALU.mult).then_inc(normed, 1)

            def split_bias(n):
                rest, part, total = biases[:, n, :], bias_part[:, :], bias_sum[:, :]
                for c in range(BIAS_PARTS):
                    then(nc.vector.tensor_copy(part, rest))
                    if c == 0:
                        then(nc.vector.tensor_scalar(total, part, ident[0:BIAS_PARTS, c:c + 1], None, ALU.mult))
                    else:
                        then(nc.vector.scalar_tensor_tensor(out=total, in0=part, scalar=ident[0:BIAS_PARTS, c:c + 1],
                                                            in1=total, op0=ALU.mult, op1=ALU.add))
                    if c < BIAS_PARTS - 1:
                        then(nc.vector.tensor_tensor(bias_rest[:, :], rest, part, ALU.subtract))
                        rest = bias_rest[:, :]
                nc.vector.tensor_copy(bias_parts[:, n, :], total).then_inc(bias_split, 1)

            dve.wait_ge(consts_made, CONSTS_MADE)
            dve.wait_ge(first_consts_loaded, 32)
            split_bias(0)
            dve.wait_ge(x_loaded[0], 16)
            for s in steps:
                blocks = slice(B * s.i, B * s.i + B)
                if s.kind == "row_add":
                    acc = row_acc[:, s.i % 2, :, :]
                    wait_loaded(dve, s.visit)
                    tile = tile_of(s.visit)
                    if s.n == 1:
                        if s.i >= 2:
                            dve.wait_ge(small_done, s.acc_free)
                        before = tile_of(s.visit - 1)
                        nc.vector.tensor_tensor(acc, before, tile, ALU.add).then_inc(rows_added, 2)
                    elif s.n:
                        dve.wait_ge(rows_added, s.visit)
                        nc.vector.tensor_tensor(acc, acc, tile, ALU.add).then_inc(rows_added, 1)
                    if s.last:
                        dve.wait_ge(rows_added, s.visit + 1)
                        then(nc.vector.tensor_tensor(acc[:, 0:2, :], acc[:, 0:2, :], acc[:, 2:4, :], ALU.add))
                        nc.vector.tensor_tensor(acc[:, 0, :], acc[:, 0, :], acc[:, 1, :], ALU.add)\
                            .then_inc(blocks_added, 1)
                elif s.kind == "fold":
                    dve.wait_ge(small_done, s.e + 1)
                    sums = small[s.bank][:, 0:B]
                    nc.vector.tensor_copy(row_sum[:, blocks], sums)
                    nc.vector.tensor_scalar(deg_in[:, blocks], sums, DEG_EPS, None, ALU.add)\
                        .then_inc(small_taken[s.bank], 1)
                elif s.kind == "layer3_degrees":
                    wait_taken(dve, s.e)
                    then(nc.vector.tensor_scalar(deg3_in[:, 0, :], row_sum[:, :], 1.0, None, ALU.add))
                    then(nc.vector.tensor_scalar(deg3_in[:, 1, :], deg3_in[:, 0, :], 0.0, None, ALU.is_gt))
                    nc.vector.tensor_scalar(deg3_in[:, 0, :], deg3_in[:, 0, :], 1e-30, None, ALU.max)\
                        .then_inc(degree3_in_ready, 1)
                    dve.wait_ge(degree3_raw, 1)
                    then(nc.vector.tensor_tensor(d3[:, :], d3[:, :], deg3_in[:, 1, :], ALU.mult))
                    dve.wait_ge(consts_loaded, CONSTS_LOADED)
                    split_bias(1)
                    split_bias(2)
                elif s.kind == "layer0_evacuate":
                    part = partial[:, s.i, :]
                    dve.wait_ge(chain_taken, s.chain_count)
                    if s.k is not None:
                        dve.wait_ge(products_done, s.k + 1)
                        nc.vector.tensor_tensor(part, banks[s.bank][:, :], part, ALU.add)\
                            .then_inc(main_taken, 1)
                        dve.wait_ge(main_taken, s.i + 1)
                    wait_taken(dve, s.e)
                    then(nc.vector.tensor_tensor(part, part, degree_rows[:, s.i, :], ALU.mult))
                    nc.vector.bn_stats(bn_stats[:, s.i, :], part).then_inc(layer0_out, 1)
                elif s.kind == "batch_norm":
                    dve.wait_ge(layer0_out, NP)
                    then(nc.vector.bn_aggr(bn_mv[:, :], bn_stats[:, :, :].rearrange("p n s -> p (n s)")))
                    nc.vector.tensor_scalar(bn_var[:, :], bn_mv[:, 1:2], BN_EPS, None, ALU.add)\
                        .then_inc(bn_variance_ready, 1)
                    dve.wait_ge(bn_rstd_ready, 1)
                    dve.wait_ge(consts_loaded, CONSTS_LOADED)
                    then(nc.vector.tensor_tensor(bn_affine[:, 0:1], bn_rstd[:, :], col_vec[:, 0:1], ALU.mult))
                    then(nc.vector.tensor_tensor(bn_affine[:, 1:2], bn_mv[:, 0:1], bn_affine[:, 0:1], ALU.mult))
                    nc.vector.tensor_tensor(bn_affine[:, 2:3], col_vec[:, 1:2], bn_affine[:, 1:2], ALU.subtract)\
                        .then_inc(bn_affine_ready, 1)
                    dve.wait_ge(small_done, s.e + 1)
                    then(nc.vector.tensor_copy(radial[:, 0:2], small[s.bank][:, P:P + 2]))
                    then(nc.vector.reciprocal(radial[:, 2:3], radial[:, 0:1]))
                    then(nc.vector.tensor_scalar(radial[:, 3:4], radial[:, 1:2], radial[:, 1:2], -2.0, ALU.mult, ALU.mult))
                    nc.vector.reciprocal(radial[:, 4:5], radial[:, 3:4]).then_inc(radial_ready, 1)
                    nc.vector.tensor_copy(bias3[:, :], small[s.bank][:, 0:P]).then_inc(small_taken[s.bank], 1)
                elif s.kind == "main_evacuate":
                    dve.wait_ge(products_done, s.k + 1)
                    if s.ev_free:
                        dve.wait_ge(small_done, s.ev_free)
                    to = sums_t[:, s.ev % 2, :]
                    if s.chain_count:
                        dve.wait_ge(chain_taken, s.chain_count)
                        nc.vector.tensor_tensor(to, banks[s.bank][:, :], partial[:, s.i, :], ALU.add)\
                            .then_inc(main_taken, 1)
                    else:
                        nc.vector.tensor_copy(to, banks[s.bank][:, :]).then_inc(main_taken, 1)
                elif s.kind == "norm":
                    xs = x[:, blocks, :]
                    if s.norm == 2:
                        dve.wait_ge(x_loaded[1], 16)
                    if s.e is not None:
                        dve.wait_ge(small_done, s.e + 1)
                        nc.vector.tensor_tensor(xs, xs, by_block(small[s.e % SMALL_BANKS][:, :]), ALU.add)\
                            .then_inc(small_taken[s.e % SMALL_BANKS], 1)
                        wait_taken(dve, s.e)
                    if s.layer == L1B:
                        wait_taken(dve, s.silu_e)
                        then(nc.vector.tensor_tensor(xs, xs, silu[:, s.silu % 2, :, :], ALU.add))
                    if s.layer == L1B:
                        if s.rows_free:
                            dve.wait_ge(small_done, s.rows_free)
                        layer_norm(s, rows[:, s.rows % 2, :, :])
                    elif s.layer == L2:
                        layer_norm(s, operand_of[L3][:, blocks, :])
                    else:
                        layer_norm(s, None)
                elif s.kind == "dense" and s.layer == L3:
                    xs = x[:, blocks, :]
                    if s.result == 0:
                        wait_taken(dve, s.bias3)
                    then(nc.vector.tensor_tensor(xs, xs, bias3[:, :].unsqueeze(1).broadcast_to([P, B, P]), ALU.add))
                    dve.wait_ge(small_done, s.e + 1)
                    if s.result >= 2:
                        dve.wait_ge(stored[s.result % 2], 16 * (s.result // 2))
                    for b in range(B):
                        n = B * s.i + b
                        last = nc.vector.scalar_tensor_tensor(
                            out=scratch[:, s.result % 2, b, :], in0=small[s.bank][:, b * P:b * P + P],
                            scalar=d3[:, n:n + 1], in1=x[:, n, :], op0=ALU.mult, op1=ALU.add)
                    last.then_inc(small_taken[s.bank], 1)
                elif s.kind == "add_ones":
                    wait_loaded(dve, s.visit)
                    for b in range(B):
                        on_diagonal = tile_of(s.visit)[:, b, b * P:b * P + P]
                        nc.vector.tensor_tensor(on_diagonal, on_diagonal, ident[:, :], ALU.add).then_inc(ones_added, 1)
                elif s.kind == "radial_newton":
                    y = recips[:, s.m % Y_SLOTS, :, :]
                    t = weights[:, s.n % S_SLOTS, :, :]
                    dve.wait_ge(recip_seeded, s.m + 1)
                    wait_slot_free(dve, s.free)
                    then(nc.vector.tensor_tensor(t, tile_of(s.visit), y, ALU.mult))
                    flat = lambda a: a.rearrange("p b n -> p (b n)")
                    nc.vector.scalar_tensor_tensor(out=flat(y), in0=flat(t), scalar=2.0, in1=flat(y),
                                                   op0=ALU.subtract, op1=ALU.mult).then_inc(recip_done, 1)
                elif s.kind == "radial_mask":
                    dve.wait_ge(exp_done, s.m + 1)
                    nc.vector.scalar_tensor_tensor(
                        out=weights[:, s.n % S_SLOTS, :, :], in0=tile_of(s.visit), scalar=CUTOFF,
                        in1=recips[:, s.m % Y_SLOTS, :, :], op0=ALU.is_lt, op1=ALU.mult).then_inc(weights_masked, 1)

        @block.tensor
        def _(pe):
            def wait_operand(made_by):
                what, n = made_by
                if what == "small":
                    wait_taken(pe, n)
                elif what == "norm":
                    pe.wait_ge(normed, n + 1)
                elif what == "pool":
                    pe.wait_ge(operand0_ready, n + 1)

            def wait_sums(ready):
                what, n = ready
                if what == "main":
                    pe.wait_ge(main_taken, n + 1)
                else:
                    pe.wait_ge(bn_applied, n)

            def add_bias(s, w):
                pe.wait_ge(bias_split, w + 1)
                nc.tensor.matmul(by_block(small[s.bank][:, :]), bf16_ones[:, :],
                                 bias_parts[:, w, :].unsqueeze(1).broadcast_to([BIAS_PARTS, B, P]),
                                 start=True, stop=False)

            pe.wait_ge(consts_made, CONSTS_MADE)
            pe.wait_ge(first_consts_loaded, 32)
            for s in steps:
                if s.bank_uses:
                    pe.wait_ge(small_taken[s.bank], s.bank_uses)
                if s.kind == "product":
                    if s.layer == L2:
                        wait_weights(pe, s.ready)
                        moving = weights[:, s.n % S_SLOTS, :, :]
                    else:
                        wait_loaded(pe, s.visit)
                        moving = tile_of(s.visit)
                    if s.layer == L3 and s.i == s.j:
                        pe.wait_ge(ones_added, B * s.ones)
                    wait_operand(s.operand)
                    group, evacuations = s.bank_free
                    if s.first and evacuations:
                        pe.wait_ge(main_taken if group == "main" else chain_taken, evacuations)
                    bank = banks[s.bank]
                    for b in range(B):
                        last = nc.tensor.matmul(bank[:, :], operand_of[s.layer][:, B * s.j + b, :], moving[:, b, :],
                                                start=s.first and b == 0, stop=s.last and b == B - 1)
                    last.then_inc(products_done, 1)
                elif s.kind == "dense":
                    if s.layer != L3:
                        add_bias(s, 1)
                    wait_sums(s.ready)
                    for b in range(B):
                        last = nc.tensor.matmul(small[s.bank][:, b * P:b * P + P],
                                                sums_t[:, s.ev % 2, b * P:b * P + P],
                                                w_sb[:, 3 if s.layer == L3 else 1, :], start=s.layer == L3,
                                                stop=s.layer == L3 or b == B - 1)
                    last.then_inc(small_done, 1)
                elif s.kind == "untranspose":
                    wait_sums(s.ready)
                    for b in range(B):
                        last = nc.tensor.transpose(small[s.bank][:, b * P:b * P + P],
                                                   sums_t[:, s.ev % 2, b * P:b * P + P], ident[:, :])
                    last.then_inc(small_done, 1)
                elif s.kind == "transpose":
                    pe.wait_ge(normed, s.norm + 1)
                    for b in range(B):
                        last = nc.tensor.transpose(small[s.bank][:, b * P:b * P + P], rows[:, s.rows % 2, b, :],
                                                   ident[:, :])
                    last.then_inc(small_done, 1)
                elif s.kind == "support":
                    w = 0 if s.layer == IN else 2
                    add_bias(s, w)
                    wait_taken(pe, s.ht_e)
                    for b in range(B):
                        last = nc.tensor.matmul(small[s.bank][:, b * P:b * P + P],
                                                rows_t[:, s.ht % 2, b * P:b * P + P], w_sb[:, w, :],
                                                start=False, stop=b == B - 1)
                    last.then_inc(small_done, 1)
                elif s.kind == "fold":
                    pe.wait_ge(blocks_added, s.i + 1)
                    for b in range(B):
                        last = nc.tensor.matmul(small[s.bank][:, b:b + 1], row_acc[:, s.i % 2, 0, b * P:b * P + P],
                                                ones[:, 0:1], start=True, stop=True)
                    last.then_inc(small_done, 1)
                elif s.kind == "degree_row":
                    pe.wait_ge(diag_ready, s.i + 1)
                    nc.tensor.matmul(small[s.bank][:, :], ones[:, :], diag[:, :, :].rearrange("p b n -> p (b n)"),
                                     start=True, stop=True).then_inc(small_done, 1)
                elif s.kind == "batch_norm":
                    pe.wait_ge(consts_loaded, CONSTS_LOADED)
                    nc.tensor.matmul(small[s.bank][:, 0:P], ones[0:1, :], biases[0:1, 3, :], start=True, stop=True)
                    nc.tensor.matmul(small[s.bank][:, P:P + 2], ones[0:1, :], radial_in[0:1, :],
                                     start=True, stop=True).then_inc(small_done, 1)


_INS = ["x", "adj", "L0_gnn_W", "L0_gnn_b", "L0_gnn_gamma", "L0_gnn_beta", "L1_gnn_W", "L1_gnn_b", "L2_gnn_W",
        "L2_gnn_B", "L2_gnn_mu", "L2_gnn_sigma", "L3_gnn_weight", "L3_gnn_bias"]
_OUTS = [((4096, 128), "float32")]


def kernel(**inputs):
    import numpy as _np
    import concourse.bacc as _bacc
    from concourse import mybir as _mybir
    from concourse.bass_utils import run_bass_kernel_spmd as _run

    nc = _bacc.Bacc("TRN2", target_bir_lowering=False, num_devices=1)
    arrays, args = {}, []
    for name in _INS:
        a = _np.ascontiguousarray(inputs[name])
        if name == "adj":
            a = _np.ascontiguousarray(a.reshape(NP, PANEL, NP, B, P).transpose(0, 2, 4, 3, 1))
        if name == "x":
            a = _np.ascontiguousarray(a.reshape(NBLK, P, P).transpose(1, 0, 2))
        arrays[f"in_{name}_dram"] = a
        args.append(nc.dram_tensor(f"in_{name}_dram", a.shape, _mybir.dt.from_np(a.dtype), kind="ExternalInput").ap())
    for i, (shape, dtype) in enumerate(_OUTS):
        dt = _mybir.dt.from_np(_np.dtype(dtype))
        args.append(nc.dram_tensor(f"out_{i}_dram", shape, dt, kind="ExternalOutput").ap())
    graph_layers_kernel(nc, *args)
    r = _run(nc, [arrays], core_ids=[0])
    got = tuple(r.results[0][f"out_{i}_dram"] for i in range(len(_OUTS)))
    return got[0]
```
